# Optimizing a Trainium2 kernel written in Bass

```python
import numpy as np
import jax
import jax.numpy as jnp

def _softmax(x, axis=-1):
    return jax.nn.softmax(x, axis=axis)

def _gelu(x):
    return jax.nn.gelu(x, approximate=True)

def _silu(x):
    return jax.nn.silu(x)

def _sigmoid(x):
    return jax.nn.sigmoid(x)

def _layernorm(x, axis=-1, eps=1e-05):
    m = jnp.mean(x, axis=axis, keepdims=True)
    v = jnp.var(x, axis=axis, keepdims=True)
    return (x - m) / jnp.sqrt(v + eps)

def _scatter_add(tgt, idx, src, axis=0):
    return tgt.at[idx].add(src)

def _segment_sum(src, seg, n):
    return jax.ops.segment_sum(src, seg, n)
kernel_name = 'mk_xattn_seq_d4_seqx_r8_f74767'

def setup_inputs(seed: int=0):
    np.random.seed(seed)
    _w = jnp.asarray

    def _rec_inputs():
        import jax
        import jax.numpy as jnp
        _rk = jax.random.key(seed)
        x = 7.22e-05 + 1 * jax.random.normal(jax.random.fold_in(_rk, 1), (32, 128, 128), jnp.float32)
        _lenS = 128 - jax.random.randint(jax.random.fold_in(_rk, 7), (32,), 0, max(1, 128 // 4) + 1, jnp.int32)
        _lenS2 = 77 - jax.random.randint(jax.random.fold_in(_rk, 8), (32,), 0, max(1, 77 // 4) + 1, jnp.int32)
        _ctx_1024P = jax.random.normal(jax.random.fold_in(_rk, 11), (32, 16, 128), jnp.float32)
        _ctx_1024c = jax.random.dirichlet(jax.random.fold_in(_rk, 511), 0.3 * jnp.ones((16,), jnp.float32), (32, 77))
        _ctx_1024t = jnp.einsum('bsk,bkd->bsd', _ctx_1024c, _ctx_1024P)
        _ctx_1024t = _ctx_1024t * jax.lax.rsqrt(jnp.mean(jnp.square(_ctx_1024t)) + 1e-12) * 0.953939
        ctx_1024 = 0.00208318 + 0.999174 * (_ctx_1024t + 0.3 * jax.random.normal(jax.random.fold_in(_rk, 611), (32, 77, 128), jnp.float32))
        return (x, ctx_1024)
    x, ctx_1024 = _rec_inputs()

    def _L0_xattn_setup():
        import jax, jax.numpy as jnp
        import numpy as np
        from functools import partial
        HEADS = 16
        DIM_HEAD = 64
        SCALE = DIM_HEAD ** (-0.5)
        MAX_ALLOWABLE = 128 * 128 * 8
        EPS = 1e-05

        def ln32(x, scale, bias):
            x32 = x.astype(jnp.float32)
            mean = jnp.mean(x32, axis=-1, keepdims=True)
            var = jnp.mean(jnp.square(x32 - mean), axis=-1, keepdims=True)
            y = (x32 - mean) * jax.lax.rsqrt(var + EPS) * scale.astype(jnp.float32) + bias.astype(jnp.float32)
            return y.astype(x.dtype)

        def heads_to_batch(t):
            b, s, d = t.shape
            return t.reshape(b, s, HEADS, d // HEADS).transpose(0, 2, 1, 3).reshape(b * HEADS, s, d // HEADS)

        def batch_to_heads(t):
            bh, s, dh = t.shape
            return t.reshape(bh // HEADS, HEADS, s, dh).transpose(0, 2, 1, 3).reshape(bh // HEADS, s, dh * HEADS)

        def _max_pow2(n):
            i = 1
            while n % 2 == 0:
                i *= 2
                n //= 2
            return i

        def sdpa(q, k, v):
            scores = jnp.einsum('bid,bjd->bij', q, k) * SCALE
            probs = jax.nn.softmax(scores, axis=2)
            return jnp.einsum('bij,bjd->bid', probs, v)

        def lowmem_attention(q, k, v):
            dimprod = q.shape[0] * q.shape[1] * k.shape[1]
            true_divisor = dimprod / MAX_ALLOWABLE
            if true_divisor < 1:
                n_splits = 1
            elif true_divisor >= q.shape[0]:
                n_splits = q.shape[0]
            else:
                nearest_pow2 = 2 ** np.round(np.log2(true_divisor))
                n_splits = int(min(_max_pow2(q.shape[0]), nearest_pow2))
            nq, nk, nv = [h.reshape(n_splits, h.shape[0] // n_splits, h.shape[-2], h.shape[-1]) for h in (q, k, v)]
            outs = jax.lax.scan(lambda c, a: (None, sdpa(*a)), None, (nq, nk, nv))[1]
            return outs.reshape(-1, outs.shape[-2], outs.shape[-1])

        def attention(x, ctx, Wq, Wkv, Wo, bo):
            q = x @ Wq
            k, v = jnp.split(ctx @ Wkv, 2, axis=-1)
            out = lowmem_attention(heads_to_batch(q), heads_to_batch(k), heads_to_batch(v))
            return batch_to_heads(out) @ Wo + bo

        def geglu_ff(x, Wff1, bff1, Wff2, bff2):
            h = x @ Wff1 + bff1
            lin, gelu = jnp.split(h, 2, axis=-1)
            h = lin * (gelu * jax.nn.sigmoid(1.702 * gelu))
            return h @ Wff2 + bff2
        key = jax.random.key(seed)
        ks = jax.random.split(key, 12)
        B, S, D, CTX = (4, 256, 128, 77)
        s = 0.02
        return {'hidden_states': jax.random.normal(ks[0], (B, S, D), jnp.float32), 'context': jax.random.normal(ks[1], (B, CTX, D), jnp.float32), 'Wq1': jax.random.normal(ks[2], (D, D), jnp.float32) * s, 'Wkv1': jax.random.normal(ks[3], (D, 2 * D), jnp.float32) * s, 'Wo1': jax.random.normal(ks[4], (D, D), jnp.float32) * s, 'bo1': jnp.zeros((D,), jnp.float32), 'Wq2': jax.random.normal(ks[5], (D, D), jnp.float32) * s, 'Wkv2': jax.random.normal(ks[6], (D, 2 * D), jnp.float32) * s, 'Wo2': jax.random.normal(ks[7], (D, D), jnp.float32) * s, 'bo2': jnp.zeros((D,), jnp.float32), 'Wff1': jax.random.normal(ks[8], (D, 8 * D), jnp.float32) * s, 'bff1': jnp.zeros((8 * D,), jnp.float32), 'Wff2': jax.random.normal(ks[9], (4 * D, D), jnp.float32) * s, 'bff2': jnp.zeros((D,), jnp.float32), 'ln1_s': jnp.ones((D,), jnp.float32), 'ln1_b': jnp.zeros((D,), jnp.float32), 'ln2_s': jnp.ones((D,), jnp.float32), 'ln2_b': jnp.zeros((D,), jnp.float32), 'ln3_s': jnp.ones((D,), jnp.float32), 'ln3_b': jnp.zeros((D,), jnp.float32)}
    _L0_xattn_all = _L0_xattn_setup()
    _L0_xattn_in = {k: v for k, v in _L0_xattn_all.items() if k in ('Wq1', 'Wkv1', 'Wo1', 'bo1', 'Wq2', 'Wkv2', 'Wo2', 'bo2', 'Wff1', 'bff1', 'Wff2', 'bff2', 'ln1_s', 'ln1_b', 'ln2_s', 'ln2_b', 'ln3_s', 'ln3_b')}
    del _L0_xattn_all

    def _L1_xattn_setup():
        import jax, jax.numpy as jnp
        import numpy as np
        D, H, E, K, DFF = (128, 16, 8, 2, 512)
        B, L, T = (4, 64, 256)
        EPS = 1e-05

        def _xavier(key, shape):
            fan_in, fan_out = (shape[-1], shape[-2])
            a = jnp.sqrt(6.0 / (fan_in + fan_out))
            return jax.random.uniform(key, shape, jnp.float32, -a, a)

        def _ln(x, g, b):
            m = x.mean(-1, keepdims=True)
            v = ((x - m) ** 2).mean(-1, keepdims=True)
            return (x - m) / jnp.sqrt(v + EPS) * g + b

        def _mha(q_in, kv_in, in_w, in_b, out_w, out_b):
            wq, wk, wv = jnp.split(in_w, 3, axis=0)
            bq, bk, bv = jnp.split(in_b, 3, axis=0)
            dh = D // H

            def heads(x, w, b):
                y = x @ w.T + b
                return y.reshape(x.shape[0], x.shape[1], H, dh).transpose(0, 2, 1, 3)
            q = heads(q_in, wq, bq)
            k = heads(kv_in, wk, bk)
            v = heads(kv_in, wv, bv)
            scores = jnp.einsum('bhqd,bhkd->bhqk', q, k) / jnp.sqrt(jnp.float32(dh))
            attn = jax.nn.softmax(scores, axis=-1)
            out = jnp.einsum('bhqk,bhkd->bhqd', attn, v)
            out = out.transpose(0, 2, 1, 3).reshape(q_in.shape[0], q_in.shape[1], D)
            return out @ out_w.T + out_b

        def _fuse_moe(x, ln_g, ln_b, rw, rb, fc1_w, fc1_b, fc2_w, fc2_b):
            h = _ln(x, ln_g, ln_b)
            logits = h @ rw.T + rb
            vals, idx = jax.lax.top_k(logits, K)
            gates = jax.nn.softmax(vals, axis=-1)
            N = x.shape[0] * x.shape[1]
            hf = h.reshape(N, D)
            h1 = jax.nn.gelu(jnp.einsum('nd,efd->enf', hf, fc1_w) + fc1_b[:, None, :], approximate=False)
            eo = jnp.einsum('enf,edf->end', h1, fc2_w) + fc2_b[:, None, :]
            idx_f = idx.reshape(N, K)
            gates_f = gates.reshape(N, K)
            gathered = eo[idx_f, jnp.arange(N)[:, None], :]
            mixed = (gathered * gates_f[..., None]).sum(axis=1).reshape(x.shape)
            return x + mixed
        key = jax.random.key(seed)
        ks = jax.random.split(key, 16)
        inp = {'latents': jax.random.normal(ks[0], (B, L, D), jnp.float32), 'tokens': jax.random.normal(ks[1], (B, T, D), jnp.float32), 'sa_ln_g': jnp.ones((D,)), 'sa_ln_b': jnp.zeros((D,)), 'sa_in_w': _xavier(ks[2], (3 * D, D)), 'sa_in_b': jnp.zeros((3 * D,)), 'sa_out_w': _xavier(ks[3], (D, D)), 'sa_out_b': jnp.zeros((D,)), 'ca_q_ln_g': jnp.ones((D,)), 'ca_q_ln_b': jnp.zeros((D,)), 'ca_kv_ln_g': jnp.ones((D,)), 'ca_kv_ln_b': jnp.zeros((D,)), 'ca_in_w': _xavier(ks[4], (3 * D, D)), 'ca_in_b': jnp.zeros((3 * D,)), 'ca_out_w': _xavier(ks[5], (D, D)), 'ca_out_b': jnp.zeros((D,)), 'moe_ln_g': jnp.ones((D,)), 'moe_ln_b': jnp.zeros((D,)), 'router_w': _xavier(ks[6], (E, D)), 'router_b': jnp.zeros((E,)), 'e_fc1_w': jax.vmap(lambda k: _xavier(k, (DFF, D)))(jax.random.split(ks[7], E)), 'e_fc1_b': jnp.zeros((E, DFF)), 'e_fc2_w': jax.vmap(lambda k: _xavier(k, (D, DFF)))(jax.random.split(ks[8], E)), 'e_fc2_b': jnp.zeros((E, D))}
        return inp
    _L1_xattn_all = _L1_xattn_setup()
    _L1_xattn_in = {k: v for k, v in _L1_xattn_all.items() if k in ('sa_ln_g', 'sa_ln_b', 'sa_in_w', 'sa_in_b', 'sa_out_w', 'sa_out_b', 'ca_q_ln_g', 'ca_q_ln_b', 'ca_kv_ln_g', 'ca_kv_ln_b', 'ca_in_w', 'ca_in_b', 'ca_out_w', 'ca_out_b', 'moe_ln_g', 'moe_ln_b', 'router_w', 'router_b', 'e_fc1_w', 'e_fc1_b', 'e_fc2_w', 'e_fc2_b')}
    del _L1_xattn_all

    def _L2_xattn_setup():
        import jax, jax.numpy as jnp
        import numpy as np
        D_MODEL = 128
        N_HEADS = 16
        D_FF = 512
        BLOCK = 64
        ROUTER_H = 128
        NEG = -1000000000.0

        def _layernorm(x, g, b, eps=1e-05):
            mu = x.mean(-1, keepdims=True)
            var = ((x - mu) ** 2).mean(-1, keepdims=True)
            return (x - mu) * jax.lax.rsqrt(var + eps) * g + b

        def _block_sparse_self_attn(x, qkv_w, sa_out_w, sa_out_b, r_w1, r_b1, r_w2, r_b2):
            B, S, D = x.shape
            H, Dh = (N_HEADS, D // N_HEADS)
            nb = S // BLOCK
            qkv = x @ qkv_w.T
            q, k, v = jnp.split(qkv, 3, axis=-1)
            q = q.reshape(B, S, H, Dh).transpose(0, 2, 1, 3)
            kh = k.reshape(B, S, H, Dh).transpose(0, 2, 1, 3)
            vh = v.reshape(B, S, H, Dh).transpose(0, 2, 1, 3)
            scores = jnp.einsum('bhqd,bhkd->bhqk', q, kh) / jnp.sqrt(jnp.float32(D))
            block_repr = k.reshape(B, nb, BLOCK, D).mean(axis=2)
            r = jax.nn.relu(block_repr @ r_w1.T + r_b1) @ r_w2.T + r_b2
            keep0 = jax.nn.sigmoid(r[0, :, 0]) > 0.5
            allowed = keep0[:, None] & keep0[None, :]
            allowed_pos = jnp.repeat(jnp.repeat(allowed, BLOCK, 0), BLOCK, 1)
            scores = jnp.where(allowed_pos[None, None], scores, NEG)
            causal = jnp.triu(jnp.ones((S, S), bool), k=1)
            scores = jnp.where(causal[None, None], -jnp.inf, scores)
            p = jax.nn.softmax(scores, axis=-1)
            out = jnp.einsum('bhqk,bhkd->bhqd', p, vh)
            out = out.transpose(0, 2, 1, 3).reshape(B, S, D)
            return out @ sa_out_w.T + sa_out_b

        def _mha_cross(q_in, kv_in, in_w, in_b, out_w, out_b):
            B, S, D = q_in.shape
            M = kv_in.shape[1]
            H, Dh = (N_HEADS, D // N_HEADS)
            wq, wk, wv = jnp.split(in_w, 3, axis=0)
            bq, bk, bv = jnp.split(in_b, 3, axis=0)
            q = (q_in @ wq.T + bq).reshape(B, S, H, Dh).transpose(0, 2, 1, 3)
            k = (kv_in @ wk.T + bk).reshape(B, M, H, Dh).transpose(0, 2, 1, 3)
            v = (kv_in @ wv.T + bv).reshape(B, M, H, Dh).transpose(0, 2, 1, 3)
            scores = jnp.einsum('bhqd,bhkd->bhqk', q, k) / jnp.sqrt(jnp.float32(Dh))
            p = jax.nn.softmax(scores, axis=-1)
            out = jnp.einsum('bhqk,bhkd->bhqd', p, v).transpose(0, 2, 1, 3).reshape(B, S, D)
            return out @ out_w.T + out_b
        key = jax.random.key(seed)
        ks = jax.random.split(key, 24)
        B, S, M, D = (2, 256, 128, D_MODEL)
        s = lambda k, shape, fan: jax.random.normal(k, shape, jnp.float32) * (1.0 / np.sqrt(fan))
        return {'tgt': jax.random.normal(ks[0], (B, S, D), jnp.float32), 'memory': jax.random.normal(ks[1], (B, M, D), jnp.float32), 'qkv_w': s(ks[2], (3 * D, D), D), 'sa_out_w': s(ks[3], (D, D), D), 'sa_out_b': jnp.zeros((D,), jnp.float32), 'r_w1': s(ks[4], (ROUTER_H, D), D), 'r_b1': jnp.zeros((ROUTER_H,), jnp.float32), 'r_w2': s(ks[5], (1, ROUTER_H), ROUTER_H), 'r_b2': jnp.zeros((1,), jnp.float32), 'ca_in_w': s(ks[6], (3 * D, D), D), 'ca_in_b': jnp.zeros((3 * D,), jnp.float32), 'ca_out_w': s(ks[7], (D, D), D), 'ca_out_b': jnp.zeros((D,), jnp.float32), 'ff_w1': s(ks[8], (D_FF, D), D), 'ff_b1': jnp.zeros((D_FF,), jnp.float32), 'ff_w2': s(ks[9], (D, D_FF), D_FF), 'ff_b2': jnp.zeros((D,), jnp.float32), 'n1_g': jnp.ones((D,), jnp.float32), 'n1_b': jnp.zeros((D,), jnp.float32), 'n2_g': jnp.ones((D,), jnp.float32), 'n2_b': jnp.zeros((D,), jnp.float32), 'n3_g': jnp.ones((D,), jnp.float32), 'n3_b': jnp.zeros((D,), jnp.float32)}
    _L2_xattn_all = _L2_xattn_setup()
    _L2_xattn_in = {k: v for k, v in _L2_xattn_all.items() if k in ('qkv_w', 'sa_out_w', 'sa_out_b', 'r_w1', 'r_b1', 'r_w2', 'r_b2', 'ca_in_w', 'ca_in_b', 'ca_out_w', 'ca_out_b', 'ff_w1', 'ff_b1', 'ff_w2', 'ff_b2', 'n1_g', 'n1_b', 'n2_g', 'n2_b', 'n3_g', 'n3_b')}
    del _L2_xattn_all

    def _L3_xattn_setup():
        import jax, jax.numpy as jnp
        import numpy as np
        E = 128
        H = 16
        D = E // H
        B, T, S = (2, 256, 256)
        SCALE = 1.0 / np.sqrt(E)

        def _layer_norm(x, g, b, eps=1e-05):
            mu = jnp.mean(x, axis=-1, keepdims=True)
            var = jnp.mean(jnp.square(x - mu), axis=-1, keepdims=True)
            return (x - mu) * jax.lax.rsqrt(var + eps) * g + b

        def _mha(h, ctx, Wq, Wk, Wv, proj_w, proj_b, causal):
            Bq, Tq, _ = h.shape
            Tk = ctx.shape[1]
            q = (h @ Wq).reshape(Bq, Tq, H, D)
            k = (ctx @ Wk).reshape(Bq, Tk, H, D)
            v = (ctx @ Wv).reshape(Bq, Tk, H, D)
            scores = jnp.einsum('bqhd,bkhd->bhqk', q, k) * SCALE
            if causal:
                mask = jnp.tril(jnp.ones((Tq, Tk), dtype=bool))
                scores = jnp.where(mask, scores, -jnp.inf)
            attn = jax.nn.softmax(scores, axis=-1)
            out = jnp.einsum('bhqk,bkhd->bqhd', attn, v).reshape(Bq, Tq, E)
            return out @ proj_w + proj_b
        key = jax.random.key(seed)
        ks = jax.random.split(key, 20)
        w = lambda k, shape: jax.random.normal(k, shape, dtype=jnp.float32) * 0.02
        inp = {'x': jax.random.normal(ks[0], (B, T, E), dtype=jnp.float32), 'context': jax.random.normal(ks[1], (B, S, E), dtype=jnp.float32), 'ln1_g': jnp.ones((E,), jnp.float32), 'ln1_b': jnp.zeros((E,), jnp.float32), 'ln2_g': jnp.ones((E,), jnp.float32), 'ln2_b': jnp.zeros((E,), jnp.float32), 'ln3_g': jnp.ones((E,), jnp.float32), 'ln3_b': jnp.zeros((E,), jnp.float32), 'Wq_s': w(ks[2], (E, E)), 'Wk_s': w(ks[3], (E, E)), 'Wv_s': w(ks[4], (E, E)), 'proj_s_w': w(ks[5], (E, E)), 'proj_s_b': jnp.zeros((E,), jnp.float32), 'Wq_c': w(ks[6], (E, E)), 'Wk_c': w(ks[7], (E, E)), 'Wv_c': w(ks[8], (E, E)), 'proj_c_w': w(ks[9], (E, E)), 'proj_c_b': jnp.zeros((E,), jnp.float32), 'w1': w(ks[10], (E, 4 * E)), 'b1': jnp.zeros((4 * E,), jnp.float32), 'w2': w(ks[11], (4 * E, E)), 'b2': jnp.zeros((E,), jnp.float32)}
        return inp
    _L3_xattn_all = _L3_xattn_setup()
    _L3_xattn_in = {k: v for k, v in _L3_xattn_all.items() if k in ('ln1_g', 'ln1_b', 'ln2_g', 'ln2_b', 'ln3_g', 'ln3_b', 'Wq_s', 'Wk_s', 'Wv_s', 'proj_s_w', 'proj_s_b', 'Wq_c', 'Wk_c', 'Wv_c', 'proj_c_w', 'proj_c_b', 'w1', 'b1', 'w2', 'b2')}
    del _L3_xattn_all
    return {'x': x, 'ctx_1024': ctx_1024, 'L0_xattn_Wq1': _L0_xattn_in['Wq1'], 'L0_xattn_Wkv1': _L0_xattn_in['Wkv1'], 'L0_xattn_Wo1': _L0_xattn_in['Wo1'], 'L0_xattn_bo1': _L0_xattn_in['bo1'], 'L0_xattn_Wq2': _L0_xattn_in['Wq2'], 'L0_xattn_Wkv2': _L0_xattn_in['Wkv2'], 'L0_xattn_Wo2': _L0_xattn_in['Wo2'], 'L0_xattn_bo2': _L0_xattn_in['bo2'], 'L0_xattn_Wff1': _L0_xattn_in['Wff1'], 'L0_xattn_bff1': _L0_xattn_in['bff1'], 'L0_xattn_Wff2': _L0_xattn_in['Wff2'], 'L0_xattn_bff2': _L0_xattn_in['bff2'], 'L0_xattn_ln1_s': _L0_xattn_in['ln1_s'], 'L0_xattn_ln1_b': _L0_xattn_in['ln1_b'], 'L0_xattn_ln2_s': _L0_xattn_in['ln2_s'], 'L0_xattn_ln2_b': _L0_xattn_in['ln2_b'], 'L0_xattn_ln3_s': _L0_xattn_in['ln3_s'], 'L0_xattn_ln3_b': _L0_xattn_in['ln3_b'], 'L1_xattn_sa_ln_g': _L1_xattn_in['sa_ln_g'], 'L1_xattn_sa_ln_b': _L1_xattn_in['sa_ln_b'], 'L1_xattn_sa_in_w': _L1_xattn_in['sa_in_w'], 'L1_xattn_sa_in_b': _L1_xattn_in['sa_in_b'], 'L1_xattn_sa_out_w': _L1_xattn_in['sa_out_w'], 'L1_xattn_sa_out_b': _L1_xattn_in['sa_out_b'], 'L1_xattn_ca_q_ln_g': _L1_xattn_in['ca_q_ln_g'], 'L1_xattn_ca_q_ln_b': _L1_xattn_in['ca_q_ln_b'], 'L1_xattn_ca_kv_ln_g': _L1_xattn_in['ca_kv_ln_g'], 'L1_xattn_ca_kv_ln_b': _L1_xattn_in['ca_kv_ln_b'], 'L1_xattn_ca_in_w': _L1_xattn_in['ca_in_w'], 'L1_xattn_ca_in_b': _L1_xattn_in['ca_in_b'], 'L1_xattn_ca_out_w': _L1_xattn_in['ca_out_w'], 'L1_xattn_ca_out_b': _L1_xattn_in['ca_out_b'], 'L1_xattn_moe_ln_g': _L1_xattn_in['moe_ln_g'], 'L1_xattn_moe_ln_b': _L1_xattn_in['moe_ln_b'], 'L1_xattn_router_w': _L1_xattn_in['router_w'], 'L1_xattn_router_b': _L1_xattn_in['router_b'], 'L1_xattn_e_fc1_w': _L1_xattn_in['e_fc1_w'], 'L1_xattn_e_fc1_b': _L1_xattn_in['e_fc1_b'], 'L1_xattn_e_fc2_w': _L1_xattn_in['e_fc2_w'], 'L1_xattn_e_fc2_b': _L1_xattn_in['e_fc2_b'], 'L2_xattn_qkv_w': _L2_xattn_in['qkv_w'], 'L2_xattn_sa_out_w': _L2_xattn_in['sa_out_w'], 'L2_xattn_sa_out_b': _L2_xattn_in['sa_out_b'], 'L2_xattn_r_w1': _L2_xattn_in['r_w1'], 'L2_xattn_r_b1': _L2_xattn_in['r_b1'], 'L2_xattn_r_w2': _L2_xattn_in['r_w2'], 'L2_xattn_r_b2': _L2_xattn_in['r_b2'], 'L2_xattn_ca_in_w': _L2_xattn_in['ca_in_w'], 'L2_xattn_ca_in_b': _L2_xattn_in['ca_in_b'], 'L2_xattn_ca_out_w': _L2_xattn_in['ca_out_w'], 'L2_xattn_ca_out_b': _L2_xattn_in['ca_out_b'], 'L2_xattn_ff_w1': _L2_xattn_in['ff_w1'], 'L2_xattn_ff_b1': _L2_xattn_in['ff_b1'], 'L2_xattn_ff_w2': _L2_xattn_in['ff_w2'], 'L2_xattn_ff_b2': _L2_xattn_in['ff_b2'], 'L2_xattn_n1_g': _L2_xattn_in['n1_g'], 'L2_xattn_n1_b': _L2_xattn_in['n1_b'], 'L2_xattn_n2_g': _L2_xattn_in['n2_g'], 'L2_xattn_n2_b': _L2_xattn_in['n2_b'], 'L2_xattn_n3_g': _L2_xattn_in['n3_g'], 'L2_xattn_n3_b': _L2_xattn_in['n3_b'], 'L3_xattn_ln1_g': _L3_xattn_in['ln1_g'], 'L3_xattn_ln1_b': _L3_xattn_in['ln1_b'], 'L3_xattn_ln2_g': _L3_xattn_in['ln2_g'], 'L3_xattn_ln2_b': _L3_xattn_in['ln2_b'], 'L3_xattn_ln3_g': _L3_xattn_in['ln3_g'], 'L3_xattn_ln3_b': _L3_xattn_in['ln3_b'], 'L3_xattn_Wq_s': _L3_xattn_in['Wq_s'], 'L3_xattn_Wk_s': _L3_xattn_in['Wk_s'], 'L3_xattn_Wv_s': _L3_xattn_in['Wv_s'], 'L3_xattn_proj_s_w': _L3_xattn_in['proj_s_w'], 'L3_xattn_proj_s_b': _L3_xattn_in['proj_s_b'], 'L3_xattn_Wq_c': _L3_xattn_in['Wq_c'], 'L3_xattn_Wk_c': _L3_xattn_in['Wk_c'], 'L3_xattn_Wv_c': _L3_xattn_in['Wv_c'], 'L3_xattn_proj_c_w': _L3_xattn_in['proj_c_w'], 'L3_xattn_proj_c_b': _L3_xattn_in['proj_c_b'], 'L3_xattn_w1': _L3_xattn_in['w1'], 'L3_xattn_b1': _L3_xattn_in['b1'], 'L3_xattn_w2': _L3_xattn_in['w2'], 'L3_xattn_b2': _L3_xattn_in['b2']}

def reference(x, ctx_1024, L0_xattn_Wq1, L0_xattn_Wkv1, L0_xattn_Wo1, L0_xattn_bo1, L0_xattn_Wq2, L0_xattn_Wkv2, L0_xattn_Wo2, L0_xattn_bo2, L0_xattn_Wff1, L0_xattn_bff1, L0_xattn_Wff2, L0_xattn_bff2, L0_xattn_ln1_s, L0_xattn_ln1_b, L0_xattn_ln2_s, L0_xattn_ln2_b, L0_xattn_ln3_s, L0_xattn_ln3_b, L1_xattn_sa_ln_g, L1_xattn_sa_ln_b, L1_xattn_sa_in_w, L1_xattn_sa_in_b, L1_xattn_sa_out_w, L1_xattn_sa_out_b, L1_xattn_ca_q_ln_g, L1_xattn_ca_q_ln_b, L1_xattn_ca_kv_ln_g, L1_xattn_ca_kv_ln_b, L1_xattn_ca_in_w, L1_xattn_ca_in_b, L1_xattn_ca_out_w, L1_xattn_ca_out_b, L1_xattn_moe_ln_g, L1_xattn_moe_ln_b, L1_xattn_router_w, L1_xattn_router_b, L1_xattn_e_fc1_w, L1_xattn_e_fc1_b, L1_xattn_e_fc2_w, L1_xattn_e_fc2_b, L2_xattn_qkv_w, L2_xattn_sa_out_w, L2_xattn_sa_out_b, L2_xattn_r_w1, L2_xattn_r_b1, L2_xattn_r_w2, L2_xattn_r_b2, L2_xattn_ca_in_w, L2_xattn_ca_in_b, L2_xattn_ca_out_w, L2_xattn_ca_out_b, L2_xattn_ff_w1, L2_xattn_ff_b1, L2_xattn_ff_w2, L2_xattn_ff_b2, L2_xattn_n1_g, L2_xattn_n1_b, L2_xattn_n2_g, L2_xattn_n2_b, L2_xattn_n3_g, L2_xattn_n3_b, L3_xattn_ln1_g, L3_xattn_ln1_b, L3_xattn_ln2_g, L3_xattn_ln2_b, L3_xattn_ln3_g, L3_xattn_ln3_b, L3_xattn_Wq_s, L3_xattn_Wk_s, L3_xattn_Wv_s, L3_xattn_proj_s_w, L3_xattn_proj_s_b, L3_xattn_Wq_c, L3_xattn_Wk_c, L3_xattn_Wv_c, L3_xattn_proj_c_w, L3_xattn_proj_c_b, L3_xattn_w1, L3_xattn_b1, L3_xattn_w2, L3_xattn_b2):
    import jax
    import jax.numpy as jnp

    def _L0_xattn_ref(hidden_states, context, Wq1, Wkv1, Wo1, bo1, Wq2, Wkv2, Wo2, bo2, Wff1, bff1, Wff2, bff2, ln1_s, ln1_b, ln2_s, ln2_b, ln3_s, ln3_b):
        import jax, jax.numpy as jnp
        import numpy as np
        from functools import partial
        HEADS = 16
        DIM_HEAD = 64
        SCALE = DIM_HEAD ** (-0.5)
        MAX_ALLOWABLE = 128 * 128 * 8
        EPS = 1e-05

        def ln32(x, scale, bias):
            x32 = x.astype(jnp.float32)
            mean = jnp.mean(x32, axis=-1, keepdims=True)
            var = jnp.mean(jnp.square(x32 - mean), axis=-1, keepdims=True)
            y = (x32 - mean) * jax.lax.rsqrt(var + EPS) * scale.astype(jnp.float32) + bias.astype(jnp.float32)
            return y.astype(x.dtype)

        def heads_to_batch(t):
            b, s, d = t.shape
            return t.reshape(b, s, HEADS, d // HEADS).transpose(0, 2, 1, 3).reshape(b * HEADS, s, d // HEADS)

        def batch_to_heads(t):
            bh, s, dh = t.shape
            return t.reshape(bh // HEADS, HEADS, s, dh).transpose(0, 2, 1, 3).reshape(bh // HEADS, s, dh * HEADS)

        def _max_pow2(n):
            i = 1
            while n % 2 == 0:
                i *= 2
                n //= 2
            return i

        def sdpa(q, k, v):
            scores = jnp.einsum('bid,bjd->bij', q, k) * SCALE
            probs = jax.nn.softmax(scores, axis=2)
            return jnp.einsum('bij,bjd->bid', probs, v)

        def lowmem_attention(q, k, v):
            dimprod = q.shape[0] * q.shape[1] * k.shape[1]
            true_divisor = dimprod / MAX_ALLOWABLE
            if true_divisor < 1:
                n_splits = 1
            elif true_divisor >= q.shape[0]:
                n_splits = q.shape[0]
            else:
                nearest_pow2 = 2 ** np.round(np.log2(true_divisor))
                n_splits = int(min(_max_pow2(q.shape[0]), nearest_pow2))
            nq, nk, nv = [h.reshape(n_splits, h.shape[0] // n_splits, h.shape[-2], h.shape[-1]) for h in (q, k, v)]
            outs = jax.lax.scan(lambda c, a: (None, sdpa(*a)), None, (nq, nk, nv))[1]
            return outs.reshape(-1, outs.shape[-2], outs.shape[-1])

        def attention(x, ctx, Wq, Wkv, Wo, bo):
            q = x @ Wq
            k, v = jnp.split(ctx @ Wkv, 2, axis=-1)
            out = lowmem_attention(heads_to_batch(q), heads_to_batch(k), heads_to_batch(v))
            return batch_to_heads(out) @ Wo + bo

        def geglu_ff(x, Wff1, bff1, Wff2, bff2):
            h = x @ Wff1 + bff1
            lin, gelu = jnp.split(h, 2, axis=-1)
            h = lin * (gelu * jax.nn.sigmoid(1.702 * gelu))
            return h @ Wff2 + bff2
        x = hidden_states
        x = attention(ln32(x, ln1_s, ln1_b), ln32(x, ln1_s, ln1_b), Wq1, Wkv1, Wo1, bo1) + x
        x = attention(ln32(x, ln2_s, ln2_b), context, Wq2, Wkv2, Wo2, bo2) + x
        x = geglu_ff(ln32(x, ln3_s, ln3_b), Wff1, bff1, Wff2, bff2) + x
        return x

    def _L1_xattn_ref(latents, tokens, sa_ln_g, sa_ln_b, sa_in_w, sa_in_b, sa_out_w, sa_out_b, ca_q_ln_g, ca_q_ln_b, ca_kv_ln_g, ca_kv_ln_b, ca_in_w, ca_in_b, ca_out_w, ca_out_b, moe_ln_g, moe_ln_b, router_w, router_b, e_fc1_w, e_fc1_b, e_fc2_w, e_fc2_b):
        import jax, jax.numpy as jnp
        import numpy as np
        D, H, E, K, DFF = (128, 16, 8, 2, 512)
        B, L, T = (4, 64, 256)
        EPS = 1e-05

        def _xavier(key, shape):
            fan_in, fan_out = (shape[-1], shape[-2])
            a = jnp.sqrt(6.0 / (fan_in + fan_out))
            return jax.random.uniform(key, shape, jnp.float32, -a, a)

        def _ln(x, g, b):
            m = x.mean(-1, keepdims=True)
            v = ((x - m) ** 2).mean(-1, keepdims=True)
            return (x - m) / jnp.sqrt(v + EPS) * g + b

        def _mha(q_in, kv_in, in_w, in_b, out_w, out_b):
            wq, wk, wv = jnp.split(in_w, 3, axis=0)
            bq, bk, bv = jnp.split(in_b, 3, axis=0)
            dh = D // H

            def heads(x, w, b):
                y = x @ w.T + b
                return y.reshape(x.shape[0], x.shape[1], H, dh).transpose(0, 2, 1, 3)
            q = heads(q_in, wq, bq)
            k = heads(kv_in, wk, bk)
            v = heads(kv_in, wv, bv)
            scores = jnp.einsum('bhqd,bhkd->bhqk', q, k) / jnp.sqrt(jnp.float32(dh))
            attn = jax.nn.softmax(scores, axis=-1)
            out = jnp.einsum('bhqk,bhkd->bhqd', attn, v)
            out = out.transpose(0, 2, 1, 3).reshape(q_in.shape[0], q_in.shape[1], D)
            return out @ out_w.T + out_b

        def _fuse_moe(x, ln_g, ln_b, rw, rb, fc1_w, fc1_b, fc2_w, fc2_b):
            h = _ln(x, ln_g, ln_b)
            logits = h @ rw.T + rb
            vals, idx = jax.lax.top_k(logits, K)
            gates = jax.nn.softmax(vals, axis=-1)
            N = x.shape[0] * x.shape[1]
            hf = h.reshape(N, D)
            h1 = jax.nn.gelu(jnp.einsum('nd,efd->enf', hf, fc1_w) + fc1_b[:, None, :], approximate=False)
            eo = jnp.einsum('enf,edf->end', h1, fc2_w) + fc2_b[:, None, :]
            idx_f = idx.reshape(N, K)
            gates_f = gates.reshape(N, K)
            gathered = eo[idx_f, jnp.arange(N)[:, None], :]
            mixed = (gathered * gates_f[..., None]).sum(axis=1).reshape(x.shape)
            return x + mixed
        q = _ln(latents, sa_ln_g, sa_ln_b)
        x = latents + _mha(q, q, sa_in_w, sa_in_b, sa_out_w, sa_out_b)
        qc = _ln(x, ca_q_ln_g, ca_q_ln_b)
        kv = _ln(tokens, ca_kv_ln_g, ca_kv_ln_b)
        x = x + _mha(qc, kv, ca_in_w, ca_in_b, ca_out_w, ca_out_b)
        return _fuse_moe(x, moe_ln_g, moe_ln_b, router_w, router_b, e_fc1_w, e_fc1_b, e_fc2_w, e_fc2_b)

    def _L2_xattn_ref(tgt, memory, qkv_w, sa_out_w, sa_out_b, r_w1, r_b1, r_w2, r_b2, ca_in_w, ca_in_b, ca_out_w, ca_out_b, ff_w1, ff_b1, ff_w2, ff_b2, n1_g, n1_b, n2_g, n2_b, n3_g, n3_b):
        import jax, jax.numpy as jnp
        import numpy as np
        D_MODEL = 128
        N_HEADS = 16
        D_FF = 512
        BLOCK = 64
        ROUTER_H = 128
        NEG = -1000000000.0

        def _layernorm(x, g, b, eps=1e-05):
            mu = x.mean(-1, keepdims=True)
            var = ((x - mu) ** 2).mean(-1, keepdims=True)
            return (x - mu) * jax.lax.rsqrt(var + eps) * g + b

        def _block_sparse_self_attn(x, qkv_w, sa_out_w, sa_out_b, r_w1, r_b1, r_w2, r_b2):
            B, S, D = x.shape
            H, Dh = (N_HEADS, D // N_HEADS)
            nb = S // BLOCK
            qkv = x @ qkv_w.T
            q, k, v = jnp.split(qkv, 3, axis=-1)
            q = q.reshape(B, S, H, Dh).transpose(0, 2, 1, 3)
            kh = k.reshape(B, S, H, Dh).transpose(0, 2, 1, 3)
            vh = v.reshape(B, S, H, Dh).transpose(0, 2, 1, 3)
            scores = jnp.einsum('bhqd,bhkd->bhqk', q, kh) / jnp.sqrt(jnp.float32(D))
            block_repr = k.reshape(B, nb, BLOCK, D).mean(axis=2)
            r = jax.nn.relu(block_repr @ r_w1.T + r_b1) @ r_w2.T + r_b2
            keep0 = jax.nn.sigmoid(r[0, :, 0]) > 0.5
            allowed = keep0[:, None] & keep0[None, :]
            allowed_pos = jnp.repeat(jnp.repeat(allowed, BLOCK, 0), BLOCK, 1)
            scores = jnp.where(allowed_pos[None, None], scores, NEG)
            causal = jnp.triu(jnp.ones((S, S), bool), k=1)
            scores = jnp.where(causal[None, None], -jnp.inf, scores)
            p = jax.nn.softmax(scores, axis=-1)
            out = jnp.einsum('bhqk,bhkd->bhqd', p, vh)
            out = out.transpose(0, 2, 1, 3).reshape(B, S, D)
            return out @ sa_out_w.T + sa_out_b

        def _mha_cross(q_in, kv_in, in_w, in_b, out_w, out_b):
            B, S, D = q_in.shape
            M = kv_in.shape[1]
            H, Dh = (N_HEADS, D // N_HEADS)
            wq, wk, wv = jnp.split(in_w, 3, axis=0)
            bq, bk, bv = jnp.split(in_b, 3, axis=0)
            q = (q_in @ wq.T + bq).reshape(B, S, H, Dh).transpose(0, 2, 1, 3)
            k = (kv_in @ wk.T + bk).reshape(B, M, H, Dh).transpose(0, 2, 1, 3)
            v = (kv_in @ wv.T + bv).reshape(B, M, H, Dh).transpose(0, 2, 1, 3)
            scores = jnp.einsum('bhqd,bhkd->bhqk', q, k) / jnp.sqrt(jnp.float32(Dh))
            p = jax.nn.softmax(scores, axis=-1)
            out = jnp.einsum('bhqk,bhkd->bhqd', p, v).transpose(0, 2, 1, 3).reshape(B, S, D)
            return out @ out_w.T + out_b
        x = _layernorm(tgt, n1_g, n1_b)
        tgt = tgt + _block_sparse_self_attn(x, qkv_w, sa_out_w, sa_out_b, r_w1, r_b1, r_w2, r_b2)
        x = _layernorm(tgt, n2_g, n2_b)
        tgt = tgt + _mha_cross(x, memory, ca_in_w, ca_in_b, ca_out_w, ca_out_b)
        x = _layernorm(tgt, n3_g, n3_b)
        ff = jax.nn.relu(x @ ff_w1.T + ff_b1) @ ff_w2.T + ff_b2
        return tgt + ff

    def _L3_xattn_ref(x, context, ln1_g, ln1_b, ln2_g, ln2_b, ln3_g, ln3_b, Wq_s, Wk_s, Wv_s, proj_s_w, proj_s_b, Wq_c, Wk_c, Wv_c, proj_c_w, proj_c_b, w1, b1, w2, b2):
        import jax, jax.numpy as jnp
        import numpy as np
        E = 128
        H = 16
        D = E // H
        B, T, S = (2, 256, 256)
        SCALE = 1.0 / np.sqrt(E)

        def _layer_norm(x, g, b, eps=1e-05):
            mu = jnp.mean(x, axis=-1, keepdims=True)
            var = jnp.mean(jnp.square(x - mu), axis=-1, keepdims=True)
            return (x - mu) * jax.lax.rsqrt(var + eps) * g + b

        def _mha(h, ctx, Wq, Wk, Wv, proj_w, proj_b, causal):
            Bq, Tq, _ = h.shape
            Tk = ctx.shape[1]
            q = (h @ Wq).reshape(Bq, Tq, H, D)
            k = (ctx @ Wk).reshape(Bq, Tk, H, D)
            v = (ctx @ Wv).reshape(Bq, Tk, H, D)
            scores = jnp.einsum('bqhd,bkhd->bhqk', q, k) * SCALE
            if causal:
                mask = jnp.tril(jnp.ones((Tq, Tk), dtype=bool))
                scores = jnp.where(mask, scores, -jnp.inf)
            attn = jax.nn.softmax(scores, axis=-1)
            out = jnp.einsum('bhqk,bkhd->bqhd', attn, v).reshape(Bq, Tq, E)
            return out @ proj_w + proj_b
        x = x + _mha(_layer_norm(x, ln1_g, ln1_b), _layer_norm(x, ln1_g, ln1_b), Wq_s, Wk_s, Wv_s, proj_s_w, proj_s_b, causal=True)
        x = x + _mha(_layer_norm(x, ln2_g, ln2_b), context, Wq_c, Wk_c, Wv_c, proj_c_w, proj_c_b, causal=False)
        h = _layer_norm(x, ln3_g, ln3_b)
        x = x + (jax.nn.gelu(h @ w1 + b1, approximate=False) @ w2 + b2)
        return x
    x = _L0_xattn_ref(x, ctx_1024, L0_xattn_Wq1, L0_xattn_Wkv1, L0_xattn_Wo1, L0_xattn_bo1, L0_xattn_Wq2, L0_xattn_Wkv2, L0_xattn_Wo2, L0_xattn_bo2, L0_xattn_Wff1, L0_xattn_bff1, L0_xattn_Wff2, L0_xattn_bff2, L0_xattn_ln1_s, L0_xattn_ln1_b, L0_xattn_ln2_s, L0_xattn_ln2_b, L0_xattn_ln3_s, L0_xattn_ln3_b)
    x = _L1_xattn_ref(x, ctx_1024, L1_xattn_sa_ln_g, L1_xattn_sa_ln_b, L1_xattn_sa_in_w, L1_xattn_sa_in_b, L1_xattn_sa_out_w, L1_xattn_sa_out_b, L1_xattn_ca_q_ln_g, L1_xattn_ca_q_ln_b, L1_xattn_ca_kv_ln_g, L1_xattn_ca_kv_ln_b, L1_xattn_ca_in_w, L1_xattn_ca_in_b, L1_xattn_ca_out_w, L1_xattn_ca_out_b, L1_xattn_moe_ln_g, L1_xattn_moe_ln_b, L1_xattn_router_w, L1_xattn_router_b, L1_xattn_e_fc1_w, L1_xattn_e_fc1_b, L1_xattn_e_fc2_w, L1_xattn_e_fc2_b)
    x = _L2_xattn_ref(x, ctx_1024, L2_xattn_qkv_w, L2_xattn_sa_out_w, L2_xattn_sa_out_b, L2_xattn_r_w1, L2_xattn_r_b1, L2_xattn_r_w2, L2_xattn_r_b2, L2_xattn_ca_in_w, L2_xattn_ca_in_b, L2_xattn_ca_out_w, L2_xattn_ca_out_b, L2_xattn_ff_w1, L2_xattn_ff_b1, L2_xattn_ff_w2, L2_xattn_ff_b2, L2_xattn_n1_g, L2_xattn_n1_b, L2_xattn_n2_g, L2_xattn_n2_b, L2_xattn_n3_g, L2_xattn_n3_b)
    x = _L3_xattn_ref(x, ctx_1024, L3_xattn_ln1_g, L3_xattn_ln1_b, L3_xattn_ln2_g, L3_xattn_ln2_b, L3_xattn_ln3_g, L3_xattn_ln3_b, L3_xattn_Wq_s, L3_xattn_Wk_s, L3_xattn_Wv_s, L3_xattn_proj_s_w, L3_xattn_proj_s_b, L3_xattn_Wq_c, L3_xattn_Wk_c, L3_xattn_Wv_c, L3_xattn_proj_c_w, L3_xattn_proj_c_b, L3_xattn_w1, L3_xattn_b1, L3_xattn_w2, L3_xattn_b2)
    return x

_drawn_inputs = setup_inputs


def setup_inputs(seed=0):
    import zlib

    import numpy as np

    out = dict(_drawn_inputs(seed))
    spreads = {'L0_xattn_bo1': (0.0, 0.1),
     'L0_xattn_bo2': (0.0, 0.1),
     'L0_xattn_bff1': (0.0, 0.355),
     'L0_xattn_bff2': (0.0, 0.1),
     'L0_xattn_ln1_s': (1.0, 0.6),
     'L0_xattn_ln1_b': (0.0, 0.437),
     'L0_xattn_ln2_s': (1.0, 0.6),
     'L0_xattn_ln2_b': (0.0, 2.0),
     'L0_xattn_ln3_s': (1.0, 0.6),
     'L0_xattn_ln3_b': (0.0, 0.695),
     'L1_xattn_sa_ln_g': (1.0, 0.2),
     'L1_xattn_sa_ln_b': (0.0, 0.1),
     'L1_xattn_sa_in_b': (0.0, 0.1),
     'L1_xattn_sa_out_b': (0.0, 0.1),
     'L1_xattn_ca_q_ln_g': (1.0, 0.6),
     'L1_xattn_ca_q_ln_b': (0.0, 0.426),
     'L1_xattn_ca_kv_ln_g': (1.0, 0.2),
     'L1_xattn_ca_kv_ln_b': (0.0, 0.1),
     'L1_xattn_ca_in_b': (0.0, 0.1),
     'L1_xattn_ca_out_b': (0.0, 0.1),
     'L1_xattn_moe_ln_g': (1.0, 0.2),
     'L1_xattn_moe_ln_b': (0.0, 0.1),
     'L1_xattn_router_b': (0.0, 0.1),
     'L1_xattn_e_fc1_b': (0.0, 0.1),
     'L1_xattn_e_fc2_b': (0.0, 0.1),
     'L2_xattn_sa_out_b': (0.0, 0.1),
     'L2_xattn_r_b1': (0.0, 0.1),
     'L2_xattn_ca_in_b': (0.0, 0.1),
     'L2_xattn_ca_out_b': (0.0, 0.1),
     'L2_xattn_ff_b1': (0.0, 0.1),
     'L2_xattn_ff_b2': (0.0, 0.1),
     'L2_xattn_n1_g': (1.0, 0.2),
     'L2_xattn_n1_b': (0.0, 0.1),
     'L2_xattn_n2_g': (1.0, 0.2),
     'L2_xattn_n2_b': (0.0, 0.423),
     'L2_xattn_n3_g': (1.0, 0.2),
     'L2_xattn_n3_b': (0.0, 0.1),
     'L3_xattn_ln1_g': (1.0, 0.6),
     'L3_xattn_ln1_b': (0.0, 2.0),
     'L3_xattn_ln2_g': (1.0, 0.6),
     'L3_xattn_ln2_b': (0.0, 0.8),
     'L3_xattn_ln3_g': (1.0, 0.6),
     'L3_xattn_ln3_b': (0.0, 0.8),
     'L3_xattn_proj_s_b': (0.0, 0.1),
     'L3_xattn_proj_c_b': (0.0, 0.1),
     'L3_xattn_b1': (0.0, 0.587),
     'L3_xattn_b2': (0.0, 0.1)}
    factors = {'L0_xattn_Wq1': 8.0,
     'L0_xattn_Wkv1': 3.095,
     'L0_xattn_Wo1': 3.103,
     'L0_xattn_Wq2': 64.0,
     'L3_xattn_Wq_s': 30.224,
     'L3_xattn_Wk_s': 30.629,
     'L3_xattn_Wq_c': 8.0,
     'L3_xattn_Wk_c': 8.0,
     'L3_xattn_Wv_c': 3.575,
     'L3_xattn_proj_c_w': 3.492}
    for name, (base, spread) in spreads.items():
        noise = np.random.default_rng([zlib.crc32(name.encode()), seed]).standard_normal(out[name].shape)
        drawn = base * np.exp(spread * noise) if base else spread * noise
        out[name] = jnp.asarray(drawn.astype(out[name].dtype))
    for name, factor in factors.items():
        out[name] = (out[name] * factor).astype(out[name].dtype)
    return out
```

```python
import concourse.bass as bass
from concourse import mybir
from contextlib import ExitStack

ALU = mybir.AluOpType
ACT = mybir.ActivationFunctionType
AX = mybir.AxisListType
F32 = mybir.dt.float32
BF16 = mybir.dt.bfloat16
U32 = mybir.dt.uint32

B, S, C, D = 32, 128, 77, 128
H, DH = 16, 8
HH = H // 2
GB = 4
NG = B // GB
T = GB * S
CT = GB * C
F = 512
NC = F // 128
E = 8
EPS = 1e-5
HIDE = -(2.0 ** 60)
NEVER = -(2.0 ** 100)
Q_PARTS = (0, 0, 0, 1, 1, 2)
K_PARTS = (0, 1, 2, 0, 1, 0)
ROWS = DH * len(Q_PARTS)
MROWS = 3

PHASES = []
for _layer in range(4):
    PHASES.append(("self", _layer))
    PHASES.append(("cross", _layer))
    PHASES.append((("geglu", "moe", "ffn", "ffn")[_layer], _layer))
SCALE_SELF = (64 ** -0.5, DH ** -0.5, D ** -0.5, D ** -0.5)
SCALE_CROSS = (64 ** -0.5, DH ** -0.5, DH ** -0.5, D ** -0.5)

ATT_COLS = 4 * D
FF_COLS = (8 * D + NC * D, E * 2 * F, 2 * F, 2 * F)
LAYER_COLS = [2 * ATT_COLS + f for f in FF_COLS]
LAYER_AT = [sum(LAYER_COLS[:l]) for l in range(5)]

COLS = {}
for _name, _n in ([(f"g{l}{k}", 1) for l in range(4) for k in "sqf"] + [(f"b{l}{k}", 1) for l in range(4) for k in "sqf"]
                  + [("g1c", 1), ("b1c", 1), ("bq1s", 1), ("bk1s", 1), ("bq1q", 1), ("bk1q", 1), ("bq2q", 1), ("bk2q", 1),
                     ("h0", 2 * NC), ("h1", E * NC), ("h2", NC), ("h3", NC), ("r1", 1), ("r2", 1),
                     ("router", E), ("iota", E), ("router_w", E)]):
    COLS[_name] = (sum(n for _, n in COLS.values()), _n)
N_COLS = sum(n for _, n in COLS.values())
ROWS_BC = ["bv1s", "bv1q", "bv2q"] + [f"bo{l}{k}" for l in range(4) for k in "sq"] + ["f0", "f2", "f3"]
TILES = ["ident", "causal", "causalT", "rw1", "rw2", "b2"]

ATT = ("self", "cross")
ALL = ("self", "cross", "geglu", "moe", "ffn")
GROWS = {}


def grows(kinds, **per):
    for name, n in per.items():
        GROWS[name] = {k: n for k in kinds}


grows(ALL, x_stats=GB, x_moments=GB, x_eps=1, x_rstd=1, x_normed=GB, xT_psum=1, xT_ready=1)
grows(ATT, q_psum=1, k_psum=1, v_psum=1, q_copied=2, k_copied=2, q_resid=1, k_resid=1, q_mid=1, k_mid=1,
      q_low=1, k_low=1, q_stacked=192, k_stacked=192, v_ready=GB,
      s_psum=4 * GB, max_read=4 * GB, m_split=3 * GB, m_parts=GB, mT_psum=GB, mT_ready=GB,
      m_stacked0=32 * GB // 2, m_stacked1=32 * GB // 2, st_psum=4 * GB, exp_done=4 * GB,
      pv_done=GB, rec_ready=GB, att_ready=GB, o_psum=GB, x_added=GB)
grows(("self", "cross", "geglu", "ffn"), xb_ready=1)
grows(("cross",), c_loaded0=8, c_loaded1=8, cT_psum=1, cT_ready=1)
grows(("geglu", "ffn", "moe"), fc1_psum=NC, hid_done=NC, y_psum=1, y_read=1)
GROWS["fc1_psum"]["moe"] = GROWS["hid_done"]["moe"] = NC * E
GROWS["y_psum"]["moe"] = E
GROWS["y_read"]["moe"] = GB * E
grows(("geglu",), gate_psum=NC, gate_done=NC)
grows(("moe",), lg_psum=1, lg_ready=1, top_vals=GB, top_idx=GB, top_diff=1, top_exp=1, gate_steps=4, coef_one=2 * GB,
      coef_ready=1, coefT_psum=1, coefT_ready=1, b2_psum=1, acc_ready=1)
CTX_NORM = ("c_stats", "c_moments", "c_eps", "c_rstd", "c_normed")
ONCE = ("mask_steps", "mask_psum", "mask_read", "mask_relu", "mask_exp")


def count(name, phase, group=0, more=0):
    per = GROWS[name]
    base = sum(NG * per.get(kind, 0) for kind, _ in PHASES[:phase])
    return base + group * per.get(PHASES[phase][0], 0) + more


class Step:

    def __init__(self, i, n0):
        self.i, self.n0, self.b = i, n0, n0 % GB

    def n(self, off=0):
        return self.n0 + off if self.i is None else self.i * (2 * GB) + (self.n0 + off)

    def g(self, off=0):
        return self.n0 // GB + off if self.i is None else self.i * 2 + (self.n0 // GB + off)

    def half(self, off=0):
        return (self.n0 + off) // 2 if self.i is None else self.i * GB + (self.n0 + off) // 2

    def has(self, off):
        return self.i is not None or 0 <= self.n0 + off < B

    def has_group(self, off):
        return self.i is not None or 0 <= self.n0 // GB + off < NG


def attention_steps(eng, emit):
    for n in range(-7, 1):
        emit(Step(None, n))
    with eng.Fori(0, 3) as i:
        for k in range(1, 2 * GB + 1):
            emit(Step(i, k))
    for n in range(3 * 2 * GB + 1, B + 1):
        emit(Step(None, n))


def feed_steps(eng, emit):
    emit(0, 0, True, False)
    with eng.Fori(0, 3) as i:
        emit(i * 2 + 1, 1, False, False)
        emit(i * 2 + 2, 0, False, False)
    emit(NG - 1, 1, False, True)


def wait(eng, sem, value):
    if not isinstance(value, int):
        assert value.min_val >= 0, (sem, value.min_val)
    if not (isinstance(value, int) and value <= 0):
        eng.wait_ge(sem, value)


def wait_alone(eng, sem, value, passed):
    wait(eng, sem, value)
    eng.sem_inc(passed, 1)


def xattn_kernel(nc, x, ctx_in, weights, cols, rows, tiles, out):
    with ExitStack() as stack:
        def sb(name, shape, dt=F32):
            return stack.enter_context(nc.sbuf_tensor(name, shape, dt))

        def psum(name):
            return stack.enter_context(nc.psum_tensor(name, [128, 512], F32))

        X = sb("X", [S, B, D])
        W = sb("W", [128, LAYER_AT[4]])
        COL = sb("COL", [128, N_COLS])
        ROW = sb("ROW", [128, len(ROWS_BC), D])
        TILE = sb("TILE", [128, len(TILES), D])
        IDENT_B = sb("IDENT_B", [128, 128], BF16)
        MASK = sb("MASK", [128, 4, 128], BF16)
        EPS4 = sb("EPS4", [128, GB])
        NHALF = sb("NHALF", [128, GB])
        EULER = sb("EULER", [128, GB])
        ST = sb("ST", [128, GB, 6])
        MV = sb("MV", [128, GB, 2])
        VE = sb("VE", [128, GB])
        RSTD = sb("RSTD", [128, GB])
        XN = sb("XN", [128, GB, D])
        XT = sb("XT", [128, 2, T])
        CST = sb("CST", [C, GB, 6])
        CMV = sb("CMV", [C, GB, 2])
        CVE = sb("CVE", [C, GB])
        CRSTD = sb("CRSTD", [C, GB])
        CX = sb("CX", [C, 2, GB, D])
        CXT = sb("CXT", [128, 2, CT])
        QF = sb("QF", [128, T])
        KF = sb("KF", [128, T])
        QP = sb("QP", [128, 3, T], BF16)
        KP = sb("KP", [128, 3, T], BF16)
        QS = sb("QS", [128, 2, HH, T], BF16)
        KS = sb("KS", [128, 2, HH, T], BF16)
        V32 = sb("V32", [128, 2, GB, H, 4 * DH])
        ONES32 = sb("ONES32", [128, 4, 4 * DH])
        XB = sb("XB", [S, 2, GB, D])
        NEGM = sb("NEGM", [S, 2, H])
        MR = sb("MR", [S, H])
        MP = sb("MP", [S, 2, 2, MROWS, HH], BF16)
        MT = sb("MT", [2 * MROWS * HH, 2, S], BF16)
        PT = sb("PT", [128, 2, H, S])
        REC = sb("REC", [D, S])
        AT = sb("AT", [D, S])
        GL = sb("GL", [128, 2, T])
        LG = sb("LG", [S, GB, E])
        TOPV = sb("TOPV", [S, GB, 8])
        TOPI = sb("TOPI", [S, GB, 8], U32)
        GATE = sb("GATE", [S, 6, GB])
        IDX = sb("IDX", [S, GB, 2])
        ONE1 = sb("ONE1", [S, GB, E])
        ONE2 = sb("ONE2", [S, GB, E])
        COEF = sb("COEF", [S, 2, GB, E])
        COEFT = sb("COEFT", [E, T])
        KM = sb("KM", [128, 2])
        KMEAN = sb("KMEAN", [128, 2])
        RH = sb("RH", [128, 2])
        RL = sb("RL", [128, 6, 2])
        KQ = sb("KQ", [128, 1])

        S_BANK = [psum("S0"), psum("S1")]
        T_BANK = [psum("T0"), psum("T1")]
        O_BANK, M_BANK = psum("OB"), psum("MB")
        A_BANK = [psum("A0"), psum("A1")]

        sem = {name: stack.enter_context(nc.semaphore(name))
               for name in [*GROWS, *CTX_NORM, *ONCE, "x_loaded", "w_loaded0", "w_loaded1", "w_loaded2", "w_loaded3",
                            "params_loaded", "consts_set", "consts_copied", "stored", "passed"]}

        def at(name, phase, group=0, more=0):
            return sem[name], count(name, phase, group, more)

        def col(name, k=0):
            c = COLS[name][0] + k
            return COL[:, c:c + 1]

        def row(name):
            return ROW[:, ROWS_BC.index(name), :]

        def tile(name):
            return TILE[:, TILES.index(name), :]

        def att_w(phase, k):
            kind, layer = PHASES[phase]
            at0 = LAYER_AT[layer] + (ATT_COLS if kind == "cross" else 0) + k * D
            return W[:, at0:at0 + D]

        def ff_w(phase, c0, n):
            at0 = LAYER_AT[PHASES[phase][1]] + 2 * ATT_COLS + c0
            return W[:, at0:at0 + n]

        def x_done(phase, group):
            if phase < 0:
                return sem["x_loaded"], 16
            return at("x_added" if PHASES[phase][0] in ATT else "y_read", phase, group)

        def letter(phase):
            return {"self": "s", "cross": "q"}.get(PHASES[phase][0], "f")

        def nk(phase):
            return S if PHASES[phase][0] == "self" else C

        def masked(phase):
            return PHASES[phase] in (("self", 2), ("self", 3))

        def biased(phase):
            return PHASES[phase] in (("self", 1), ("cross", 1), ("cross", 2))

        def normed_ctx(phase):
            return PHASES[phase] == ("cross", 1)

        block = stack.enter_context(nc.Block())

        @block.sync
        def _(sp):
            sp.dma_start(X[:, :, :], x.rearrange("b s d -> s b d")).then_inc(sem["x_loaded"], 16)
            sp.dma_start(COL[:, :], cols).then_inc(sem["params_loaded"], 16)
            sp.dma_start(ROW[:, :, :], rows).then_inc(sem["params_loaded"], 16)
            sp.dma_start(TILE[:, :, :], tiles).then_inc(sem["params_loaded"], 16)
            for layer in range(4):
                a, z = LAYER_AT[layer], LAYER_AT[layer + 1]
                sp.dma_start(W[:, a:z], weights[:, a:z]).then_inc(sem[f"w_loaded{layer}"], 16)
            sp.wait_ge(sem["consts_set"], 9)

            def attention(phase):
                cross = PHASES[phase][0] == "cross"

                def stack_parts(s, src, dst, parts, width, par):
                    for r, part in enumerate(parts):
                        for hh in range(2):
                            sp.dma_start(dst[64 * hh + DH * r:64 * hh + DH * (r + 1), par, :, 0:width],
                                         src[64 * hh:64 * hh + 64, part, 0:width]).then_inc(s, 16)

                def emit(st):
                    par = st.n0 // GB % 2
                    if cross and st.b == 1 and st.has_group(2):
                        wait(sp, *at("cT_psum", phase, st.g(1)))
                        sp.dma_start(CX[:, par, :, :], ctx_in[bass.ds(st.g(2) * GB, GB)].rearrange("b s d -> s b d"))\
                          .then_inc(sem[f"c_loaded{par}"], 16)
                    if st.has(1):
                        p1 = (st.n0 + 1) % 2
                        g1, b1 = (st.n0 + 1) // GB, (st.n0 + 1) % GB
                        wait(sp, *at("mT_ready", phase, 0, st.n(2)))
                        for hh in range(2):
                            sp.dma_start(QS[64 * hh + ROWS:64 * hh + ROWS + MROWS, g1 % 2, :, b1 * S:(b1 + 1) * S],
                                         MT[hh * MROWS * HH:(hh + 1) * MROWS * HH, p1, :])\
                              .then_inc(sem[f"m_stacked{p1}"], 16)
                    if st.b == 0 and st.has_group(1):
                        wait_alone(sp, *at("st_psum", phase, st.g(0)), sem["passed"])
                        wait_alone(sp, *at("s_psum", phase, st.g(0)), sem["passed"])
                        wait(sp, *at("q_low", phase, st.g(2)))
                        stack_parts(sem["q_stacked"], QP, QS, Q_PARTS, T, 1 - par)
                        wait(sp, *at("k_low", phase, st.g(2)))
                        stack_parts(sem["k_stacked"], KP, KS, K_PARTS, CT if cross else T, 1 - par)

                attention_steps(sp, emit)

            def store(phase):
                def emit(g, par, first, last):
                    wait(sp, *x_done(phase, g + 1))
                    sp.dma_start(out[bass.ds(g * GB, GB)].rearrange("b s d -> s b d") if not isinstance(g, int)
                                 else out[g * GB:(g + 1) * GB].rearrange("b s d -> s b d"),
                                 X[:, bass.ds(g * GB, GB), :] if not isinstance(g, int)
                                 else X[:, g * GB:(g + 1) * GB, :]).then_inc(sem["stored"], 16)
                feed_steps(sp, emit)
                sp.wait_ge(sem["stored"], 16 * NG)

            for phase, (kind, _) in enumerate(PHASES):
                if kind in ATT:
                    attention(phase)
            store(len(PHASES) - 1)

        @block.gpsimd
        def _(pool):
            nc.gpsimd.memset(EPS4[:, :], EPS).then_inc(sem["consts_set"], 1)
            nc.gpsimd.memset(NHALF[:, :], -0.5).then_inc(sem["consts_set"], 1)
            nc.gpsimd.memset(EULER[:, :], 2.718281828459045).then_inc(sem["consts_set"], 1)
            nc.gpsimd.memset(V32[:, :, :, :, :], 0.0).then_inc(sem["consts_set"], 1)
            nc.gpsimd.memset(ONES32[:, :, :], 0.0).then_inc(sem["consts_set"], 1)
            for par in range(2):
                nc.gpsimd.memset(KS[:, par, :, :], 1.0).then_inc(sem["consts_set"], 1)
                nc.gpsimd.memset(QS[:, par, :, :], 0.0).then_inc(sem["consts_set"], 1)
            pool.wait_ge(sem["consts_set"], 9)
            for r in range(4):
                nc.gpsimd.memset(ONES32[:, r, r * DH:(r + 1) * DH], 1.0).then_inc(sem["consts_set"], 1)
            pool.wait_ge(sem["params_loaded"], 48)
            pool.wait_ge(sem["x_loaded"], 16)

            def rstd(phase, g):
                wait(pool, *at("x_moments", phase, g + 1))
                wait(pool, *at("x_normed", phase, g))
                nc.gpsimd.tensor_tensor(VE[:, :], MV[:, :, 1], EPS4[:, :], ALU.add).then_inc(sem["x_eps"], 1)
                wait(pool, *at("x_eps", phase, g + 1))
                nc.gpsimd.tensor_tensor(RSTD[:, :], VE[:, :], NHALF[:, :], ALU.pow).then_inc(sem["x_rstd"], 1)

            def add_out_bias(phase, g, par, bias):
                wait(pool, *x_done(phase - 1, g + 1))
                if PHASES[phase][0] not in ATT:
                    wait(pool, *x_done(phase, g - 1))
                nc.gpsimd.tensor_tensor(
                    XB[:, par, :, :], X[:, bass.ds(g * GB, GB), :] if not isinstance(g, int) else X[:, g * GB:(g + 1) * GB, :],
                    bias.unsqueeze(1).to_broadcast([S, GB, D]), ALU.add).then_inc(sem["xb_ready"], 1)

            def attention(phase):
                kind, layer = PHASES[phase]
                width = T if kind == "self" else CT

                def emit(st):
                    par = st.n0 // GB % 2
                    if st.b == 1 and st.has_group(2):
                        rstd(phase, st.g(2))
                        if normed_ctx(phase):
                            pool.wait_ge(sem["c_moments"], GB * st.g(2) + GB)
                            wait(pool, sem["c_normed"], GB * st.g(2))
                            nc.gpsimd.tensor_tensor(CVE[:, :], CMV[:, :, 1], EPS4[0:C, :], ALU.add).then_inc(sem["c_eps"], 1)
                            pool.wait_ge(sem["c_eps"], st.g(2) + 1)
                            nc.gpsimd.tensor_tensor(CRSTD[:, :], CVE[:, :], NHALF[0:C, :], ALU.pow).then_inc(sem["c_rstd"], 1)
                    if st.has(1):
                        p1 = (st.n0 + 1) % 2
                        wait(pool, *at("max_read", phase, 0, 4 * st.n(2)))
                        wait_alone(pool, *at("mT_psum", phase, 0, st.n(0)), sem["passed"])
                        negm = NEGM[:, p1, :].rearrange("p (a h) -> p a h", a=2)
                        mr = MR[:, :].rearrange("p (a h) -> p a h", a=2)
                        nc.gpsimd.tensor_copy(MP[:, p1, :, 0, :], negm).then_inc(sem["m_split"], 1)
                        wait(pool, *at("m_split", phase, 0, 3 * st.n(1) + 1))
                        nc.gpsimd.tensor_tensor(mr, negm, MP[:, p1, :, 0, :], ALU.subtract).then_inc(sem["m_split"], 1)
                        wait_alone(pool, *at("m_split", phase, 0, 3 * st.n(1) + 2), sem["passed"])
                        nc.gpsimd.tensor_copy(MP[:, p1, :, 1, :], mr).then_inc(sem["m_split"], 1)
                        wait(pool, *at("m_split", phase, 0, 3 * st.n(1) + 3))
                        nc.gpsimd.tensor_tensor(MP[:, p1, :, 2, :], mr, MP[:, p1, :, 1, :], ALU.subtract)\
                          .then_inc(sem["m_parts"], 1)
                    if st.b == 3 and st.has_group(2):
                        for f, p, w, c in ((QF, QP, T, "q"), (KF, KP, width, "k")):
                            wait(pool, *at(f"{c}_copied", phase, st.g(3)))
                            nc.gpsimd.tensor_tensor(f[:, 0:w], f[:, 0:w], p[:, 0, 0:w], ALU.subtract)\
                              .then_inc(sem[f"{c}_resid"], 1)
                    if st.b == 0 and st.has_group(1):
                        for f, p, w, c in ((QF, QP, T, "q"), (KF, KP, width, "k")):
                            wait(pool, *at(f"{c}_mid", phase, st.g(2)))
                            nc.gpsimd.tensor_tensor(p[:, 2, 0:w], f[:, 0:w], p[:, 1, 0:w], ALU.subtract)\
                              .then_inc(sem[f"{c}_low"], 1)
                    if st.b == 1 and st.has_group(0):
                        add_out_bias(phase, st.g(0), par, row(f"bo{layer}{letter(phase)}"))

                attention_steps(pool, emit)

            def feed(phase):
                kind, layer = PHASES[phase]
                def gates(g):
                    wait(pool, *at("top_diff", phase, g + 1))
                    wait(pool, *at("gate_steps", phase, g))
                    nc.gpsimd.tensor_tensor(GATE[:, 1, :], EULER[:, :], GATE[:, 0, :], ALU.pow).then_inc(sem["top_exp"], 1)

                rstd(phase, 0)
                if kind == "moe":
                    gates(0)

                def emit(g, par, first, last):
                    if not last:
                        rstd(phase, g + 1)
                    if kind != "moe":
                        add_out_bias(phase, g, par, row(f"f{layer}"))
                    elif not last:
                        gates(g + 1)
                feed_steps(pool, emit)

            for phase, (kind, _) in enumerate(PHASES):
                (attention if kind in ATT else feed)(phase)

        @block.vector
        def _(dve):
            dve.wait_ge(sem["params_loaded"], 48)
            dve.wait_ge(sem["x_loaded"], 16)
            dve.wait_ge(sem["consts_set"], 13)
            nc.vector.tensor_copy(IDENT_B[:, :], tile("ident")).then_inc(sem["consts_copied"], 1)
            nc.vector.tensor_copy(MASK[:, 0, :], tile("causal")).then_inc(sem["consts_copied"], 1)
            nc.vector.tensor_copy(MASK[:, 1, :], tile("causalT")).then_inc(sem["consts_copied"], 1)

            def xs(g, b=None):
                if b is None:
                    return X[:, g * GB:(g + 1) * GB, :] if isinstance(g, int) else X[:, bass.ds(g * GB, GB), :]
                n = g * GB + b
                return X[:, n:n + 1, :] if isinstance(n, int) else X[:, bass.ds(n, 1), :]

            def moments(phase, g):
                wait(dve, *x_done(phase - 1, g + 1))
                wait(dve, *at("x_rstd", phase, g))
                for b in range(GB):
                    nc.vector.bn_stats(ST[:, b, :], xs(g, b)).then_inc(sem["x_stats"], 1)
                for b in range(GB):
                    wait_alone(dve, *at("x_stats", phase, g, b + 1), sem["passed"])
                    nc.vector.bn_aggr(MV[:, b, :], ST[:, b, :]).then_inc(sem["x_moments"], 1)

            def normalise(phase, g):
                wait(dve, *at("x_rstd", phase, g + 1))
                wait(dve, *at("xT_psum", phase, g))
                for b in range(GB):
                    nc.vector.tensor_scalar(XN[:, b:b + 1, :], xs(g, b), MV[:, b, 0:1], RSTD[:, b:b + 1],
                                            ALU.subtract, ALU.mult).then_inc(sem["x_normed"], 1)

            def ctx_moments(phase, st, par):
                dve.wait_ge(*at(f"c_loaded{par}", phase, 0, 16 * (st.g(2) // 2 + 1) if st.i is None
                                else 16 * (st.i + st.n0 // GB // 2 + 2)))
                wait(dve, sem["c_rstd"], st.g(2))
                for b in range(GB):
                    nc.vector.bn_stats(CST[:, b, :], CX[:, par, b, :]).then_inc(sem["c_stats"], 1)
                for b in range(GB):
                    wait_alone(dve, sem["c_stats"], GB * st.g(2) + b + 1, sem["passed"])
                    nc.vector.bn_aggr(CMV[:, b, :], CST[:, b, :]).then_inc(sem["c_moments"], 1)

            def v_columns(keys, par):
                return bass.AP(tensor=V32[:, :, :, :, :].tensor, offset=par * GB * H * 4 * DH,
                               ap=[[2 * GB * H * 4 * DH, keys], [16 * DH, GB * H // 4], [5 * DH, 4], [1, DH]])

            def block_router(phase):
                n = [0]

                def done(ins):
                    n[0] += 1
                    ins.then_inc(sem["mask_steps"], 1)
                    dve.wait_ge(sem["mask_steps"], n[0])

                dve.wait_ge(*at("k_psum", phase, 1))
                done(nc.vector.tensor_reduce(KM[:, :], A_BANK[0][:, 0:S].rearrange("p (a t) -> p a t", a=2), AX.X, ALU.add))
                done(nc.vector.tensor_scalar(KMEAN[:, :], KM[:, :], 1.0 / 64, None, ALU.mult))
                dve.wait_ge(sem["mask_psum"], 2)
                done(nc.vector.tensor_scalar(RL[:, 0, :], M_BANK[:, 0:2], col("r2"), None, ALU.add))
                dve.wait_ge(sem["mask_exp"], 1)
                done(nc.vector.tensor_scalar(RL[:, 2, :], RL[:, 1, :], 1.0, None, ALU.add))
                done(nc.vector.reciprocal(RL[:, 3, :], RL[:, 2, :]))
                done(nc.vector.tensor_scalar(RL[:, 4, :], RL[:, 3, :], 0.5, None, ALU.is_gt))
                done(nc.vector.tensor_copy(KQ[0:64, :], RL[0:64, 4, 0:1]))
                done(nc.vector.tensor_copy(KQ[64:128, :], RL[64:128, 4, 1:2]))
                done(nc.vector.tensor_scalar(RL[:, 5, :], RL[:, 4, :], KQ[:, 0:1], None, ALU.mult))
                done(nc.vector.tensor_scalar(RL[:, 2, :], RL[:, 5, :], 1.0, -HIDE, ALU.subtract, ALU.mult))
                for m, name in ((2, "causal"), (3, "causalT")):
                    for j in range(2):
                        done(nc.vector.tensor_scalar(MASK[:, m, 64 * j:64 * j + 64], tile(name)[:, 64 * j:64 * j + 64],
                                                     RL[:, 2, j:j + 1], None, ALU.add))

            MASK_STEPS = 14

            def attention(phase):
                kind, layer = PHASES[phase]
                cross = kind == "cross"
                keys = nk(phase)

                def emit(st):
                    par = st.n0 // GB % 2

                    def row_max(u):
                        p2 = st.n0 % 2
                        if u == 0:
                            wait(dve, *at("m_parts", phase, 0, st.n(1)))
                        wait(dve, *at("s_psum", phase, 0, 4 * st.n(2) + u + 1))
                        nc.vector.tensor_reduce(NEGM[:, p2, 4 * u:4 * u + 4],
                                                S_BANK[u % 2][:, 0:4 * keys].rearrange("p (h k) -> p h k", h=4),
                                                AX.X, ALU.max, negate=True).then_inc(sem["max_read"], 1)

                    if st.b == 1 and st.has_group(2):
                        moments(phase, st.g(2))
                        if normed_ctx(phase):
                            ctx_moments(phase, st, par)
                    if st.b == 2 and st.has_group(2):
                        normalise(phase, st.g(2))
                        if normed_ctx(phase):
                            dve.wait_ge(sem["c_rstd"], st.g(2) + 1)
                            for b in range(GB):
                                nc.vector.tensor_scalar(CX[:, par, b, :], CX[:, par, b, :], CMV[:, b, 0:1], CRSTD[:, b:b + 1],
                                                        ALU.subtract, ALU.mult).then_inc(sem["c_normed"], 1)
                    if st.has(2):
                        row_max(0)
                    if st.has(-1):
                        wait(dve, *at("pv_done", phase, 0, st.n(0)))
                        nc.vector.reciprocal(REC[:, :], O_BANK[:, S:2 * S]).then_inc(sem["rec_ready"], 1)
                        wait(dve, *at("rec_ready", phase, 0, st.n(0)))
                        wait(dve, *at("o_psum", phase, 0, st.n(-1)))
                        nc.vector.tensor_tensor(AT[:, :], O_BANK[:, 0:S], REC[:, :], ALU.mult).then_inc(sem["att_ready"], 1)
                    if st.has(2):
                        row_max(1)
                    if st.b == 3 and st.has_group(2) and layer == 2 and kind == "self" and st.i is None and st.n0 < -4:
                        block_router(phase)
                    if st.b == 0 and st.has_group(1):
                        for f, p, w, c in ((QF, QP, T, "q"), (KF, KP, GB * keys, "k")):
                            wait(dve, *at(f"{c}_resid", phase, st.g(2)))
                            nc.vector.tensor_copy(p[:, 1, 0:w], f[:, 0:w]).then_inc(sem[f"{c}_mid"], 1)
                        wait(dve, *at("v_psum", phase, st.g(2)))
                        wait(dve, *at("pv_done", phase, st.g(0)))
                        vb = A_BANK[0 if cross else 1][0:keys, :].rearrange("p (c r e) -> p c r e", r=4, e=DH)
                        v32 = v_columns(keys, 1 - par)
                        if biased(phase):
                            bias = row(f"bv{layer}{letter(phase)}")[0:keys, :].rearrange("p (c r e) -> p c r e", r=4, e=DH)
                            for b in range(GB):
                                nc.vector.tensor_tensor(v32[:, 4 * b:4 * b + 4], vb[:, 4 * b:4 * b + 4], bias, ALU.add)\
                                  .then_inc(sem["v_ready"], 1)
                        else:
                            for b in range(0, GB, 2):
                                nc.vector.tensor_copy(v32[:, 4 * b:4 * b + 8], vb[:, 4 * b:4 * b + 8])\
                                  .then_inc(sem["v_ready"], 2)
                    if st.has(1):
                        p1 = (st.n0 + 1) % 2
                        wait(dve, *at("mT_psum", phase, 0, st.n(2)))
                        wait(dve, *at(f"m_stacked{p1}", phase, 0, 32 * st.half(1)))
                        nc.vector.tensor_copy(MT[:, p1, :], M_BANK[0:2 * MROWS * HH, 0:S // 2].bitcast(BF16))\
                          .then_inc(sem["mT_ready"], 1)
                    if st.has(2):
                        row_max(2)
                        row_max(3)
                    if st.has(-1):
                        gp, bp = (st.n0 - 1) // GB % 2, (st.n0 - 1) % GB
                        wait(dve, *at("o_psum", phase, 0, st.n(0)))
                        wait(dve, *at("xb_ready", phase, st.g(1) if st.b else st.g(0)))
                        n1 = st.n(-1)
                        dst = X[:, n1:n1 + 1, :] if isinstance(n1, int) else X[:, bass.ds(n1, 1), :]
                        nc.vector.tensor_tensor(dst, M_BANK[:, 0:D].unsqueeze(1), XB[:, gp, bp:bp + 1, :], ALU.add)\
                          .then_inc(sem["x_added"], 1)

                attention_steps(dve, emit)

            def feed(phase):
                kind, layer = PHASES[phase]
                moments(phase, 0)
                normalise(phase, 0)

                def route(g, par):
                    wait(dve, *at("lg_psum", phase, g + 1))
                    rb = COL[:, COLS["router"][0]:COLS["router"][0] + E].unsqueeze(1).to_broadcast([S, GB, E])
                    nc.vector.tensor_tensor(LG[:, :, :], A_BANK[1][:, 0:GB * E].rearrange("p (b e) -> p b e", b=GB), rb, ALU.add)\
                      .then_inc(sem["lg_ready"], 1)
                    wait_alone(dve, *at("lg_ready", phase, g + 1), sem["passed"])
                    for b in range(GB):
                        nc.vector.max(TOPV[:, b, :], LG[:, b, :]).then_inc(sem["top_vals"], 1)
                    for b in range(GB):
                        wait_alone(dve, *at("top_vals", phase, g, b + 1), sem["passed"])
                        nc.vector.max_index(TOPI[:, b, :], TOPV[:, b, :], LG[:, b, :]).then_inc(sem["top_idx"], 1)
                    wait(dve, *at("top_exp", phase, g))
                    nc.vector.tensor_tensor(GATE[:, 0, :], TOPV[:, :, 1], TOPV[:, :, 0], ALU.subtract).then_inc(sem["top_diff"], 1)
                    wait(dve, *at("top_idx", phase, g + 1))
                    nc.vector.tensor_copy(IDX[:, :, :], TOPI[:, :, 0:2]).then_inc(sem["gate_steps"], 1)
                    wait(dve, *at("top_exp", phase, g + 1))
                    nc.vector.tensor_scalar(GATE[:, 2, :], GATE[:, 1, :], 1.0, None, ALU.add).then_inc(sem["gate_steps"], 1)
                    wait(dve, *at("gate_steps", phase, g, 2))
                    nc.vector.reciprocal(GATE[:, 3, :], GATE[:, 2, :]).then_inc(sem["gate_steps"], 1)
                    wait(dve, *at("gate_steps", phase, g, 3))
                    nc.vector.tensor_tensor(GATE[:, 4, :], GATE[:, 1, :], GATE[:, 3, :], ALU.mult).then_inc(sem["gate_steps"], 1)
                    wait(dve, *at("gate_steps", phase, g, 4))
                    iota = COL[:, COLS["iota"][0]:COLS["iota"][0] + E]
                    for b in range(GB):
                        nc.vector.tensor_scalar(ONE1[:, b, :], iota, IDX[:, b, 0:1], GATE[:, 3, b:b + 1],
                                                ALU.is_equal, ALU.mult).then_inc(sem["coef_one"], 1)
                        nc.vector.tensor_scalar(ONE2[:, b, :], iota, IDX[:, b, 1:2], GATE[:, 4, b:b + 1],
                                                ALU.is_equal, ALU.mult).then_inc(sem["coef_one"], 1)
                    wait(dve, *at("coef_one", phase, g + 1))
                    nc.vector.tensor_tensor(COEF[:, par, :, :], ONE1[:, :, :], ONE2[:, :, :], ALU.add)\
                      .then_inc(sem["coef_ready"], 1)

                def route_sum(g, par):
                    wait(dve, *at("coefT_psum", phase, g + 1))
                    nc.vector.tensor_copy(COEFT[:, :], A_BANK[1][0:E, :]).then_inc(sem["coefT_ready"], 1)
                    wait(dve, *at("b2_psum", phase, g + 1))
                    nc.vector.tensor_tensor(XB[:, par, :, :], A_BANK[1][:, :].rearrange("p (b d) -> p b d", b=GB), xs(g), ALU.add)\
                      .then_inc(sem["acc_ready"], 1)

                def mix(g, e, par):
                    wait(dve, *at("y_psum", phase, g, e + 1))
                    wait(dve, *at("acc_ready", phase, g + 1))
                    bank = (O_BANK, M_BANK)[e % 2]
                    for b in range(GB):
                        if e:
                            wait(dve, *at("y_read", phase, g, GB * (e - 1) + b + 1))
                        nc.vector.scalar_tensor_tensor(
                            xs(g, b) if e == E - 1 else XB[:, par, b:b + 1, :],
                            bank[:, b * D:(b + 1) * D].unsqueeze(1), COEF[:, par, b, e:e + 1], XB[:, par, b:b + 1, :],
                            ALU.mult, ALU.add).then_inc(sem["y_read"], 1)

                if kind == "moe":
                    route(0, 0)
                    route_sum(0, 0)

                def emit_moe(g, par, first, last):
                    for e in range(E):
                        if e == 1 and not last:
                            moments(phase, g + 1)
                        if e == 2 and not last:
                            normalise(phase, g + 1)
                        if e == 4 and not last:
                            route(g + 1, 1 - par)
                        if e == 6 and not last:
                            route_sum(g + 1, 1 - par)
                        if e:
                            mix(g, e - 1, par)
                        elif not first:
                            mix(g - 1, E - 1, 1 - par)
                    if last:
                        mix(g, E - 1, par)

                def finish(g, par):
                    wait(dve, *at("y_psum", phase, g + 1))
                    wait(dve, *at("xb_ready", phase, g + 1))
                    nc.vector.tensor_tensor(xs(g), (O_BANK, M_BANK)[par][:, :].rearrange("p (b d) -> p b d", b=GB),
                                            XB[:, par, :, :], ALU.add).then_inc(sem["y_read"], 1)

                def emit(g, par, first, last):
                    if kind == "geglu":
                        wait(dve, *at("y_psum", phase, g - 1))
                        for c in range(NC):
                            wait(dve, *at("fc1_psum", phase, g, c + 1))
                            wait(dve, *at("gate_done", phase, g, c + 1))
                            nc.vector.scalar_tensor_tensor(
                                PT[:, par, 4 * c:4 * c + 4, :].rearrange("p h s -> p (h s)"), S_BANK[c % 2][:, :], col("h0", c),
                                GL[:, c % 2, :], ALU.add, ALU.mult).then_inc(sem["hid_done"], 1)
                    if not last:
                        moments(phase, g + 1)
                        normalise(phase, g + 1)
                    if not first:
                        finish(g - 1, 1 - par)
                    if last:
                        finish(g, par)

                feed_steps(dve, emit_moe if kind == "moe" else emit)

            for phase, (kind, _) in enumerate(PHASES):
                (attention if kind in ATT else feed)(phase)

        @block.scalar
        def _(act):
            act.wait_ge(sem["params_loaded"], 48)

            def turned(phase, g, par):
                k = f"{PHASES[phase][1]}{letter(phase)}"
                wait(act, *at("xT_psum", phase, g + 1))
                if PHASES[phase][0] in ATT:
                    wait(act, *at("v_psum", phase, g - 1))
                else:
                    wait(act, *at("y_psum", phase, g - 1))
                nc.scalar.activation(XT[:, par, :], A_BANK[0][:, :], ACT.Identity, bias=col("b" + k), scale=col("g" + k))\
                  .then_inc(sem["xT_ready"], 1)

            def attention(phase):
                kind, layer = PHASES[phase]
                cross = kind == "cross"
                scale = (SCALE_CROSS if cross else SCALE_SELF)[layer]
                keys = nk(phase)

                def emit(st):
                    par = st.n0 // GB % 2

                    def exps(u):
                        if u == 0:
                            wait(act, *at("pv_done", phase, 0, st.n(-1)))
                        wait(act, *at("st_psum", phase, 0, 4 * st.n() + u + 1))
                        nc.scalar.activation(PT[0:keys, st.n0 % 2, 4 * u:4 * u + 4, :].rearrange("p h s -> p (h s)"),
                                             T_BANK[u % 2][0:keys, :], ACT.Exp, scale=scale).then_inc(sem["exp_done"], 1)

                    if st.b == 2 and st.has_group(2):
                        turned(phase, st.g(2), par)
                        if cross:
                            wait(act, *at("cT_psum", phase, st.g(3)))
                            if normed_ctx(phase):
                                nc.scalar.activation(CXT[:, par, :], A_BANK[1][:, 0:CT], ACT.Identity,
                                                     bias=col("b1c"), scale=col("g1c")).then_inc(sem["cT_ready"], 1)
                            else:
                                nc.scalar.activation(CXT[:, par, :], A_BANK[1][:, 0:CT], ACT.Copy).then_inc(sem["cT_ready"], 1)
                    if st.has(0):
                        exps(0)
                        exps(1)
                    if st.b == 3 and st.has_group(2):
                        for f, p, w, c, bank in ((QF, QP, T, "q", A_BANK[0 if cross else 1]),
                                                 (KF, KP, GB * keys, "k", A_BANK[1 if cross else 0])):
                            wait(act, *at(f"{c}_psum", phase, st.g(3)))
                            wait(act, *at(f"{c}_low", phase, st.g(2)))
                            wait(act, *at(f"{c}_stacked", phase, st.g(2)))
                            if c == "k" and layer == 2 and kind == "self" and st.i is None and st.n0 < -4:
                                act.wait_ge(sem["mask_steps"], 1)
                            bias = col(f"b{c}{layer}{letter(phase)}") if biased(phase) else 0.0
                            nc.scalar.activation(f[:, 0:w], bank[:, 0:w], ACT.Identity, bias=bias).then_inc(sem[f"{c}_copied"], 1)
                            nc.scalar.activation(p[:, 0, 0:w], bank[:, 0:w], ACT.Identity, bias=bias).then_inc(sem[f"{c}_copied"], 1)
                        if layer == 2 and kind == "self" and st.i is None and st.n0 < -4:
                            act.wait_ge(sem["mask_psum"], 1)
                            nc.scalar.activation(RH[:, :], M_BANK[:, 0:2], ACT.Relu, bias=col("r1")).then_inc(sem["mask_relu"], 1)
                            act.wait_ge(sem["mask_steps"], 3)
                            nc.scalar.activation(RL[:, 1, :], RL[:, 0, :], ACT.Exp, scale=-1.0).then_inc(sem["mask_exp"], 1)
                    if st.has(0):
                        exps(2)
                    if st.has(0):
                        exps(3)

                attention_steps(act, emit)

            def feed(phase):
                kind, layer = PHASES[phase]
                func = {"geglu": ACT.Gelu_apprx_sigmoid, "moe": ACT.Gelu}.get(kind, ACT.Relu if layer == 2 else ACT.Gelu)
                turned(phase, 0, 0)

                def hidden(g, e, par):
                    unit = e if kind == "moe" else 0
                    up = e % 2 if kind == "moe" else par
                    wait(act, *at("y_psum", phase, g, unit - 1))
                    for c in range(NC):
                        wait(act, *at("fc1_psum", phase, g, NC * unit + c + 1))
                        nc.scalar.activation(PT[:, up, 4 * c:4 * c + 4, :].rearrange("p h s -> p (h s)"),
                                             (T_BANK[0], S_BANK[0], T_BANK[1], S_BANK[1])[c][:, :], func,
                                             bias=col(f"h{layer}", NC * e + c)).then_inc(sem["hid_done"], 1)

                def emit(g, par, first, last):
                    if kind == "geglu":
                        for c in range(NC):
                            wait(act, *at("gate_psum", phase, g, c + 1))
                            wait(act, *at("hid_done", phase, g, c - 1))
                            nc.scalar.activation(GL[:, c % 2, :], T_BANK[c % 2][:, :], func, bias=col("h0", NC + c))\
                              .then_inc(sem["gate_done"], 1)
                    elif kind == "ffn":
                        hidden(g, 0, par)
                    else:
                        for e in range(E):
                            hidden(g, e, par)
                            if e == 2 and not last:
                                turned(phase, g + 1, 1 - par)
                    if kind != "moe" and not last:
                        turned(phase, g + 1, 1 - par)

                feed_steps(act, emit)

            for phase, (kind, _) in enumerate(PHASES):
                (attention if kind in ATT else feed)(phase)

        @block.tensor
        def _(pe):
            pe.wait_ge(sem["params_loaded"], 48)
            pe.wait_ge(sem["consts_copied"], 3)
            ident = tile("ident")

            def turn(phase, g):
                wait(pe, *at("x_normed", phase, g + 1))
                for b in range(GB):
                    last = nc.tensor.transpose(A_BANK[0][:, b * S:(b + 1) * S], XN[:, b, :], ident)
                last.then_inc(sem["xT_psum"], 1)

            def attention(phase):
                kind, layer = PHASES[phase]
                cross = kind == "cross"
                keys = nk(phase)
                mask = 2 if layer == 2 else 0

                def emit(st):
                    par = st.n0 // GB % 2

                    def scores(u):
                        hh, h0 = u // 2, 4 * (u % 2)
                        g2, b2 = (st.n0 + 2) // GB % 2, (st.n0 + 2) % GB
                        if u == 0 and b2 == 0:
                            g = st.g(1)
                            wait(pe, *at("q_stacked", phase, g + 1))
                            wait(pe, *at("k_stacked", phase, g + 1))
                        wait(pe, *at("max_read", phase, 0, 4 * st.n(2) + u - 1))
                        bank = S_BANK[u % 2]
                        if masked(phase):
                            nc.tensor.matmul(bank[:, :].rearrange("p (h k) -> p h k", h=4), IDENT_B[:, :],
                                             MASK[:, mask, :].unsqueeze(1).to_broadcast([S, 4, S]),
                                             start=True, stop=False, skip_group_check=True)
                        for j in range(4):
                            last = nc.tensor.matmul(bank[:, j * keys:(j + 1) * keys],
                                                    QS[64 * hh:64 * hh + ROWS, g2, h0 + j, b2 * S:(b2 + 1) * S],
                                                    KS[64 * hh:64 * hh + ROWS, g2, h0 + j, b2 * keys:(b2 + 1) * keys],
                                                    start=not masked(phase), stop=True, skip_group_check=True)
                        last.then_inc(sem["s_psum"], 1)

                    def scores_t(u):
                        hh, h0 = u // 2, 4 * (u % 2)
                        if u == 0:
                            wait(pe, *at(f"m_stacked{st.n0 % 2}", phase, 0, 32 * (st.half() + 1)))
                        wait(pe, *at("exp_done", phase, 0, 4 * st.n() + u - 1))
                        bank = T_BANK[u % 2]
                        if masked(phase):
                            nc.tensor.matmul(bank[:, :].rearrange("p (h k) -> p h k", h=4), IDENT_B[:, :],
                                             MASK[:, mask + 1, :].unsqueeze(1).to_broadcast([S, 4, S]),
                                             start=True, stop=False, skip_group_check=True)
                        for j in range(4):
                            last = nc.tensor.matmul(bank[0:keys, j * S:(j + 1) * S],
                                                    KS[64 * hh:64 * hh + ROWS + MROWS, par, h0 + j, st.b * keys:(st.b + 1) * keys],
                                                    QS[64 * hh:64 * hh + ROWS + MROWS, par, h0 + j, st.b * S:(st.b + 1) * S],
                                                    start=not masked(phase), stop=True, skip_group_check=True)
                        last.then_inc(sem["st_psum"], 1)

                    if st.b == 2 and st.has_group(2):
                        if cross:
                            wait(pe, *at("v_ready", phase, st.g(2)))
                        else:
                            wait(pe, *at("k_copied", phase, st.g(2)))
                        turn(phase, st.g(2))
                        if cross:
                            wait(pe, *at("k_copied", phase, st.g(2)))
                            if normed_ctx(phase):
                                pe.wait_ge(sem["c_normed"], GB * (st.g(2) + 1))
                            else:
                                value = st.g(2) // 2 + 1 if st.i is None else st.i + (st.n0 // GB // 2 + 2)
                                pe.wait_ge(*at(f"c_loaded{par}", phase, 0, value * 16))
                            for b in range(GB):
                                last = nc.tensor.transpose(A_BANK[1][:, b * C:(b + 1) * C], CX[:, par, b, :], ident[0:C, 0:C])
                            last.then_inc(sem["cT_psum"], 1)
                    if st.b == 3 and st.has_group(2):
                        wait(pe, *at("xT_ready", phase, st.g(3)))
                        if not cross:
                            wait(pe, *at("v_ready", phase, st.g(2)))
                        nc.tensor.matmul(A_BANK[0 if cross else 1][:, :], att_w(phase, 0), XT[:, par, :],
                                         start=True, stop=True).then_inc(sem["q_psum"], 1)
                        if cross:
                            wait(pe, *at("cT_ready", phase, st.g(3)))
                        src = CXT[:, par, :] if cross else XT[:, par, :]
                        nc.tensor.matmul(A_BANK[1 if cross else 0][:, 0:GB * keys], att_w(phase, 1), src,
                                         start=True, stop=True).then_inc(sem["k_psum"], 1)
                        if layer == 2 and kind == "self" and st.i is None and st.n0 < -4:
                            pe.wait_ge(sem["mask_steps"], 2)
                            nc.tensor.matmul(M_BANK[:, 0:2], tile("rw1"), KMEAN[:, :], start=True, stop=True)\
                              .then_inc(sem["mask_psum"], 1)
                            pe.wait_ge(sem["mask_relu"], 1)
                            nc.tensor.matmul(M_BANK[:, 0:2], tile("rw2"), RH[:, :], start=True, stop=True)\
                              .then_inc(sem["mask_psum"], 1)
                            pe.wait_ge(sem["mask_steps"], 14)
                    if st.b == 0 and st.has_group(1):
                        wait(pe, *at("q_copied", phase, st.g(2)))
                        src = CXT if cross else XT
                        for b in range(GB):
                            last = nc.tensor.matmul(A_BANK[0 if cross else 1][0:keys, b * D:(b + 1) * D],
                                                    src[:, 1 - par, b * keys:(b + 1) * keys], att_w(phase, 2),
                                                    start=True, stop=True, skip_group_check=True)
                        last.then_inc(sem["v_psum"], 1)
                    if st.has(0):
                        scores_t(0)
                    if st.has(2):
                        scores(0)
                    if st.has(-1):
                        gp, bp = (st.n0 - 1) // GB % 2, (st.n0 - 1) % GB
                        wait(pe, *at("exp_done", phase, 0, 4 * st.n()))
                        wait(pe, *at("v_ready", phase, st.g(1) if st.b else st.g(0)))
                        wait(pe, *at("att_ready", phase, 0, st.n(-1)))
                        for products in (True, False):
                            for r in range(4):
                                for j in range(4):
                                    h = 4 * j + r
                                    left = V32[0:keys, gp, bp, h, :] if products else ONES32[0:keys, r, :]
                                    at0 = 0 if products else S
                                    last = nc.tensor.matmul(O_BANK[4 * DH * j:4 * DH * (j + 1), at0:at0 + S], left,
                                                            PT[0:keys, (st.n0 - 1) % 2, h, :],
                                                            start=r == 0, stop=r == 3, skip_group_check=True)
                        last.then_inc(sem["pv_done"], 1)
                    if st.has(0):
                        scores_t(1)
                    if st.has(2):
                        scores(1)
                    if st.has(1):
                        p1 = (st.n0 + 1) % 2
                        wait(pe, *at("m_parts", phase, 0, st.n(2)))
                        wait_alone(pe, *at("x_added", phase, 0, st.n(-1)), sem["passed"])
                        nc.tensor.transpose(M_BANK[0:2 * MROWS * HH, 0:S // 2].bitcast(BF16),
                                            MP[:, p1, :, :, :].rearrange("p a m h -> p (a m h)"), IDENT_B[:, :])\
                          .then_inc(sem["mT_psum"], 1)
                    if st.has(0):
                        scores_t(2)
                    if st.has(2):
                        scores(2)
                    if st.has(0):
                        scores_t(3)
                    if st.has(2):
                        scores(3)
                    if st.has(-1):
                        wait(pe, *at("att_ready", phase, 0, st.n()))
                        wait(pe, *at("mT_ready", phase, 0, st.n(2) if st.has(1) else B))
                        nc.tensor.matmul(M_BANK[:, 0:D], AT[:, :], att_w(phase, 3), start=True, stop=True)\
                          .then_inc(sem["o_psum"], 1)

                attention_steps(pe, emit)

            def feed(phase):
                kind, layer = PHASES[phase]

                def route(g, par):
                    wait(pe, *at("xT_ready", phase, g + 1))
                    wait(pe, *at("acc_ready", phase, g))
                    for b in range(GB):
                        last = nc.tensor.matmul(A_BANK[1][:, b * E:(b + 1) * E], XT[:, par, b * S:(b + 1) * S],
                                                ff_router, start=True, stop=True, skip_group_check=True)
                    last.then_inc(sem["lg_psum"], 1)

                def route_turn(g, par):
                    wait(pe, *at("coef_ready", phase, g + 1))
                    for b in range(GB):
                        last = nc.tensor.transpose(A_BANK[1][0:E, b * S:(b + 1) * S], COEF[:, par, b, :], ident)
                    last.then_inc(sem["coefT_psum"], 1)

                def route_bias(g):
                    wait(pe, *at("coefT_ready", phase, g + 1))
                    for b in range(GB):
                        last = nc.tensor.matmul(A_BANK[1][:, b * D:(b + 1) * D], COEFT[:, b * S:(b + 1) * S], tile("b2")[0:E, :],
                                                start=True, stop=True, skip_group_check=True)
                    last.then_inc(sem["b2_psum"], 1)

                def fc1(g, e, par):
                    unit = e if kind == "moe" else 0
                    wait(pe, *at("xT_ready", phase, g + 1))
                    for c in range(NC):
                        if kind == "geglu":
                            wait(pe, *at("gate_done", phase, g, c - 1))
                            nc.tensor.matmul(T_BANK[c % 2][:, :], ff_w(phase, F + c * 128, 128), XT[:, par, :],
                                             start=True, stop=True).then_inc(sem["gate_psum"], 1)
                            wait(pe, *at("hid_done", phase, g, c - 1))
                            nc.tensor.matmul(S_BANK[c % 2][:, :], ff_w(phase, c * 128, 128), XT[:, par, :],
                                             start=True, stop=True).then_inc(sem["fc1_psum"], 1)
                        else:
                            wait(pe, *at("hid_done", phase, g, NC * unit + c - NC + 1))
                            nc.tensor.matmul((T_BANK[0], S_BANK[0], T_BANK[1], S_BANK[1])[c][:, :],
                                             ff_w(phase, e * 2 * F + c * 128, 128), XT[:, par, :],
                                             start=True, stop=True).then_inc(sem["fc1_psum"], 1)

                def fc2(g, e, par):
                    unit = e if kind == "moe" else 0
                    up = e % 2 if kind == "moe" else par
                    first_col = (2 * F if kind == "geglu" else e * 2 * F + F)
                    wait(pe, *at("hid_done", phase, g, NC * (unit + 1)))
                    if kind == "moe":
                        wait(pe, *at("y_read", phase, g, GB * (unit - 1)))
                    elif kind == "ffn":
                        wait(pe, *at("y_read", phase, g - 1))
                    for b in range(GB):
                        for c in range(NC):
                            last = nc.tensor.matmul((O_BANK, M_BANK)[up][:, b * D:(b + 1) * D],
                                                    PT[:, up, 4 * c + b, :],
                                                    ff_w(phase, first_col + c * D, D), start=c == 0, stop=c == NC - 1,
                                                    skip_group_check=True)
                    last.then_inc(sem["y_psum"], 1)

                ff_router = COL[:, COLS["router_w"][0]:COLS["router_w"][0] + E]
                turn(phase, 0)
                if kind == "moe":
                    route(0, 0)
                    route_turn(0, 0)
                    route_bias(0)

                def emit(g, par, first, last):
                    for e in range(E if kind == "moe" else 1):
                        fc1(g, e, par)
                        if not last and (kind != "moe" or e == 2):
                            wait(pe, *at("xT_ready", phase, g + 1))
                            turn(phase, g + 1)
                        if not last and kind == "moe":
                            if e == 4:
                                route(g + 1, 1 - par)
                            if e == 5:
                                route_turn(g + 1, 1 - par)
                            if e == 6:
                                route_bias(g + 1)
                        if e:
                            fc2(g, e - 1, par)
                        elif not first:
                            fc2(g - 1, E - 1 if kind == "moe" else 0, 1 - par)
                    if last:
                        fc2(g, E - 1 if kind == "moe" else 0, par)

                feed_steps(pe, emit)

            for phase, (kind, layer) in enumerate(PHASES):
                if kind == "self":
                    pe.wait_ge(sem[f"w_loaded{layer}"], 16)
                wait(pe, *x_done(phase - 1, NG))
                (attention if kind in ATT else feed)(phase)


def kernel(**inputs):
    import numpy as np
    import concourse.bacc as bacc
    from concourse.bass_utils import run_bass_kernel_spmd

    a = {k: np.asarray(v) for k, v in inputs.items()}
    L = [lambda name, l=l: a[f"L{l}_xattn_{name}"] for l in range(4)]
    order = np.array([(hh * HH + h) * DH + d for hh in range(2) for d in range(DH) for h in range(HH)])

    def att(wq, wk, wv, wo):
        return [wq[:, order], wk[:, order], wv, wo]

    def chunks(w):
        return w.reshape(NC, 128, D).transpose(1, 0, 2).reshape(128, NC * D)

    def in_proj(w):
        return [w[i * D:(i + 1) * D].T for i in range(3)]

    w = []
    w += att(L[0]("Wq1"), L[0]("Wkv1")[:, :D], L[0]("Wkv1")[:, D:], L[0]("Wo1"))
    w += att(L[0]("Wq2"), L[0]("Wkv2")[:, :D], L[0]("Wkv2")[:, D:], L[0]("Wo2"))
    w += [L[0]("Wff1"), chunks(L[0]("Wff2"))]
    w += att(*in_proj(L[1]("sa_in_w")), L[1]("sa_out_w").T)
    w += att(*in_proj(L[1]("ca_in_w")), L[1]("ca_out_w").T)
    for e in range(E):
        w += [L[1]("e_fc1_w")[e].T, chunks(L[1]("e_fc2_w")[e].T)]
    w += att(*in_proj(L[2]("qkv_w")), L[2]("sa_out_w").T)
    w += att(*in_proj(L[2]("ca_in_w")), L[2]("ca_out_w").T)
    w += [L[2]("ff_w1").T, chunks(L[2]("ff_w2").T)]
    w += att(L[3]("Wq_s"), L[3]("Wk_s"), L[3]("Wv_s"), L[3]("proj_s_w"))
    w += att(L[3]("Wq_c"), L[3]("Wk_c"), L[3]("Wv_c"), L[3]("proj_c_w"))
    w += [L[3]("w1"), chunks(L[3]("w2"))]

    cols = np.zeros((128, N_COLS), np.float32)

    def put(name, v):
        c, n = COLS[name]
        cols[:, c:c + n] = v.reshape(n, 128).T

    for l, (g, b) in enumerate((("ln1_s ln2_s ln3_s", "ln1_b ln2_b ln3_b"), ("sa_ln_g ca_q_ln_g moe_ln_g", "sa_ln_b ca_q_ln_b moe_ln_b"),
                                ("n1_g n2_g n3_g", "n1_b n2_b n3_b"), ("ln1_g ln2_g ln3_g", "ln1_b ln2_b ln3_b"))):
        for k, gn, bn in zip("sqf", g.split(), b.split()):
            put(f"g{l}{k}", L[l](gn))
            put(f"b{l}{k}", L[l](bn))
    put("g1c", L[1]("ca_kv_ln_g"))
    put("b1c", L[1]("ca_kv_ln_b"))
    for tag, bias in (("1s", L[1]("sa_in_b")), ("1q", L[1]("ca_in_b")), ("2q", L[2]("ca_in_b"))):
        put("bq" + tag, bias[:D][order])
        put("bk" + tag, bias[D:2 * D][order])
    put("h0", L[0]("bff1"))
    put("h1", L[1]("e_fc1_b"))
    put("h2", L[2]("ff_b1"))
    put("h3", L[3]("b1"))
    put("r1", L[2]("r_b1"))
    put("r2", np.broadcast_to(L[2]("r_b2"), (128,)))
    put("router", np.repeat(L[1]("router_b"), 128))
    put("iota", np.repeat(np.arange(E, dtype=np.float32), 128))
    put("router_w", L[1]("router_w"))

    bias_rows = {"bv1s": L[1]("sa_in_b")[2 * D:], "bv1q": L[1]("ca_in_b")[2 * D:], "bv2q": L[2]("ca_in_b")[2 * D:],
                 "bo0s": L[0]("bo1"), "bo0q": L[0]("bo2"), "bo1s": L[1]("sa_out_b"), "bo1q": L[1]("ca_out_b"),
                 "bo2s": L[2]("sa_out_b"), "bo2q": L[2]("ca_out_b"), "bo3s": L[3]("proj_s_b"), "bo3q": L[3]("proj_c_b"),
                 "f0": L[0]("bff2"), "f2": L[2]("ff_b2"), "f3": L[3]("b2")}
    rows = np.ascontiguousarray(np.broadcast_to(np.stack([bias_rows[n] for n in ROWS_BC]), (128, len(ROWS_BC), D)))
    at = np.arange(128)
    tiles = np.zeros((128, len(TILES), D), np.float32)
    tiles[:, 0] = np.eye(128)
    tiles[:, 1] = np.where(at[None, :] > at[:, None], NEVER, 0.0)
    tiles[:, 2] = tiles[:, 1].T
    tiles[:, 3] = L[2]("r_w1").T[order]
    tiles[:, 4] = np.broadcast_to(L[2]("r_w2").reshape(128, 1), (128, 128))
    tiles[:E, 5] = L[1]("e_fc2_b")

    arrays = {"x": a["x"], "ctx": a["ctx_1024"], "weights": np.concatenate(w, axis=1), "cols": cols, "rows": rows, "tiles": tiles}
    nc = bacc.Bacc("TRN2", target_bir_lowering=False, num_devices=1)
    args = []
    for name in arrays:
        arrays[name] = np.ascontiguousarray(arrays[name])
        args.append(nc.dram_tensor(name, arrays[name].shape, mybir.dt.from_np(arrays[name].dtype), kind="ExternalInput").ap())
    out = nc.dram_tensor("out", (B, S, D), F32, kind="ExternalOutput").ap()
    xattn_kernel(nc, *args, out)
    r = run_bass_kernel_spmd(nc, [arrays], core_ids=[0])
    return r.results[0]["out"]
```

```python
import concourse.bass as bass
from concourse import mybir
from contextlib import ExitStack

ALU = mybir.AluOpType
ACT = mybir.ActivationFunctionType
AX = mybir.AxisListType
F32 = mybir.dt.float32
BF16 = mybir.dt.bfloat16
U32 = mybir.dt.uint32

B, S, C, D = 32, 128, 77, 128
H, DH = 16, 8
HH = H // 2
GB = 4
NG = B // GB
T = GB * S
CT = GB * C
F = 512
NC = F // 128
E = 8
EPS = 1e-5
HIDE = -(2.0 ** 60)
NEVER = -(2.0 ** 100)
Q_PARTS = (0, 0, 0, 1, 1, 2)
K_PARTS = (0, 1, 2, 0, 1, 0)
ROWS = DH * len(Q_PARTS)
MROWS = 3

PHASES = []
for _layer in range(4):
    PHASES.append(("self", _layer))
    PHASES.append(("cross", _layer))
    PHASES.append((("geglu", "moe", "ffn", "ffn")[_layer], _layer))
SCALE_SELF = (64 ** -0.5, DH ** -0.5, D ** -0.5, D ** -0.5)
SCALE_CROSS = (64 ** -0.5, DH ** -0.5, DH ** -0.5, D ** -0.5)

ATT_COLS = 4 * D
FF_COLS = (8 * D + NC * D, E * 2 * F, 2 * F, 2 * F)
LAYER_COLS = [2 * ATT_COLS + f for f in FF_COLS]
LAYER_AT = [sum(LAYER_COLS[:l]) for l in range(5)]

COLS = {}
for _name, _n in ([(f"g{l}{k}", 1) for l in range(4) for k in "sqf"] + [(f"b{l}{k}", 1) for l in range(4) for k in "sqf"]
                  + [("g1c", 1), ("b1c", 1), ("bq1s", 1), ("bk1s", 1), ("bq1q", 1), ("bk1q", 1), ("bq2q", 1), ("bk2q", 1),
                     ("h0", 2 * NC), ("h1", E * NC), ("h2", NC), ("h3", NC), ("r1", 1), ("r2", 1),
                     ("router", E), ("iota", E), ("router_w", E)]):
    COLS[_name] = (sum(n for _, n in COLS.values()), _n)
N_COLS = sum(n for _, n in COLS.values())
ROWS_BC = ["bv1s", "bv1q", "bv2q"] + [f"bo{l}{k}" for l in range(4) for k in "sq"] + ["f0", "f2", "f3"]
TILES = ["ident", "causal", "causalT", "rw1", "rw2", "b2"]

ATT = ("self", "cross")
ALL = ("self", "cross", "geglu", "moe", "ffn")
GROWS = {}


def grows(kinds, **per):
    for name, n in per.items():
        GROWS[name] = {k: n for k in kinds}


grows(ALL, x_stats=GB, x_moments=GB, x_eps=1, x_rstd=1, x_normed=GB, xT_psum=1, xT_ready=1)
grows(ATT, q_psum=1, k_psum=1, v_psum=1, q_copied=2, k_copied=2, q_resid=1, k_resid=1, q_mid=1, k_mid=1,
      q_low=1, k_low=1, q_stacked0=96, k_stacked0=96, q_stacked1=96, k_stacked1=96, v_ready=GB, sums_done=GB,
      s_psum=4 * GB, max_read=4 * GB, m_split=3 * GB, m_parts=GB, mT_psum=GB, mT_ready=GB,
      m_stacked00=16 * GB // 2, m_stacked01=16 * GB // 2, m_stacked10=16 * GB // 2, m_stacked11=16 * GB // 2, st_psum=4 * GB, exp_done=4 * GB,
      pv_done=GB, rec_ready=GB, att_ready=GB, o_psum=GB, x_added=GB)
grows(("self", "cross", "geglu", "ffn"), xb_ready=1)
grows(("cross",), c_loaded0=8, c_loaded1=8, cT_psum=1, cT_ready=1)
grows(("geglu", "ffn", "moe"), fc1_psum=NC, hid_done=NC, y_psum=1, y_read=1)
GROWS["fc1_psum"]["moe"] = GROWS["hid_done"]["moe"] = NC * E
GROWS["y_psum"]["moe"] = E
GROWS["y_read"]["moe"] = GB * E
grows(("geglu",), gate_psum=NC, gate_done=NC)
grows(("moe",), lg_psum=1, lg_ready=1, top_vals=GB, top_idx=GB, top_diff=1, top_exp=1, gate_steps=4, coef_one=2 * GB,
      coef_ready=1, coefT_psum=1, coefT_ready=1, b2_psum=1, acc_ready=1)
CTX_NORM = ("c_stats", "c_moments", "c_eps", "c_rstd", "c_normed")
ONCE = ("mask_steps", "mask_psum", "mask_relu", "mask_exp")


FIRST = {"pv_done": 1, "x_added": 1, "y_psum": 1, "y_read": 1}


def count(name, phase, group=0, more=0):
    per = GROWS[name]
    base = FIRST.get(name, 0) + sum(NG * per.get(kind, 0) for kind, _ in PHASES[:phase])
    return base + group * per.get(PHASES[phase][0], 0) + more


class Step:

    def __init__(self, phase, i, n0):
        self.phase, self.i, self.n0, self.b = phase, i, n0, n0 % GB
        self.chained = PHASES[phase][0] == "self"

    def batch(self, off=0):
        if self.i is not None:
            return self.phase, self.i * (2 * GB) + (self.n0 + off)
        n = self.n0 + off
        return (self.phase, n) if n < B or not self.chained else (self.phase + 1, n - B)

    def group(self, off=0):
        if self.i is not None:
            return self.phase, self.i * 2 + (self.n0 // GB + off)
        g = self.n0 // GB + off
        return (self.phase, g) if g < NG or not self.chained else (self.phase + 1, g - NG)

    def pairs(self, off=0):
        phase, n = self.batch(off)
        return phase, n // 2 if self.i is None else self.i * GB + (self.n0 + off) // 2

    def ctx_pair(self):
        return self.group(2)[1] // 2 if self.i is None else self.i + (self.n0 // GB + 2) // 2

    def has(self, off):
        return self.i is not None or (0 <= self.n0 + off and (self.n0 + off < B or self.chained))

    def has_group(self, off):
        return self.i is not None or (0 <= self.n0 // GB + off and (self.n0 // GB + off < NG or self.chained))

    def feeds(self, n):
        return self.i is None and not self.chained and self.n0 == n

    def routes_blocks(self):
        return self.i is None and self.n0 == 2 - 2 * GB and PHASES[self.phase] == ("self", 2)


LEAD_IN = (-10, -7, -6, -5, -4)


def attention_steps(eng, emit, phase):
    if PHASES[phase][0] == "self":
        for n in (*(() if phase else LEAD_IN), *range(LEAD_IN[-1] + 1, 1)):
            emit(Step(phase, None, n))
    with eng.Fori(0, 2) as i:
        for k in range(1, 2 * GB + 1):
            emit(Step(phase, i, k))
    for n in range(2 * 2 * GB + 1, B + 1):
        emit(Step(phase, None, n))


def lead_in(emit, phase, *steps):
    if phase + 1 < len(PHASES):
        for k in steps:
            emit(Step(phase + 1, None, LEAD_IN[k]))


def feed_steps(eng, emit):
    emit(0, 0, True, False)
    with eng.Fori(0, 3) as i:
        emit(i * 2 + 1, 1, False, False)
        emit(i * 2 + 2, 0, False, False)
    emit(NG - 1, 1, False, True)


def wait(eng, sem, value):
    if not isinstance(value, int):
        assert value.min_val > 0, (sem, value.min_val)
    if not (isinstance(value, int) and value <= 0):
        eng.wait_ge(sem, value)


def wait_alone(eng, sem, value, passed):
    wait(eng, sem, value)
    eng.sem_inc(passed, 1)


def xattn_kernel(nc, x, ctx_in, weights, cols, rows, tiles, out):
    with ExitStack() as stack:
        def sb(name, shape, dt=F32):
            return stack.enter_context(nc.sbuf_tensor(name, shape, dt))

        def psum(name):
            return stack.enter_context(nc.psum_tensor(name, [128, 512], F32))

        X = sb("X", [S, B, D])
        W = sb("W", [128, LAYER_AT[4]])
        COL = sb("COL", [128, N_COLS])
        ROW = sb("ROW", [128, len(ROWS_BC), D])
        TILE = sb("TILE", [128, len(TILES), D])
        IDENT_B = sb("IDENT_B", [128, 128], BF16)
        MASK = sb("MASK", [128, 4, 128], BF16)
        EPS4 = sb("EPS4", [128, GB])
        NHALF = sb("NHALF", [128, GB])
        EULER = sb("EULER", [128, GB])
        ST = sb("ST", [128, GB, 6])
        MV = sb("MV", [128, GB, 2])
        VE = sb("VE", [128, GB])
        RSTD = sb("RSTD", [128, GB])
        XN = sb("XN", [128, GB, D])
        XT = sb("XT", [128, 2, T])
        CST = sb("CST", [C, GB, 6])
        CMV = sb("CMV", [C, GB, 2])
        CVE = sb("CVE", [C, GB])
        CRSTD = sb("CRSTD", [C, GB])
        CX = sb("CX", [C, 2, GB, D])
        CXT = sb("CXT", [128, 2, CT])
        QF = sb("QF", [128, T])
        KF = sb("KF", [128, T])
        QP = sb("QP", [128, 3, T], BF16)
        KP = sb("KP", [128, 3, T], BF16)
        QS = sb("QS", [128, 2, HH, T], BF16)
        KS = sb("KS", [128, 2, HH, T], BF16)
        V32 = sb("V32", [128, 2, GB, H, 4 * DH])
        ONES32 = sb("ONES32", [128, 4, 4 * DH])
        XB = sb("XB", [S, 2, GB, D])
        NEGM = sb("NEGM", [S, 2, H])
        MR = sb("MR", [S, H])
        MP = sb("MP", [S, 2, 2, MROWS, HH], BF16)
        MT = sb("MT", [2 * MROWS * HH, 2, S], BF16)
        PT = sb("PT", [128, 2, H, S])
        REC = sb("REC", [D, S])
        AT = sb("AT", [D, S])
        GL = sb("GL", [128, 2, T])
        LG = sb("LG", [S, GB, E])
        TOPV = sb("TOPV", [S, GB, 8])
        TOPI = sb("TOPI", [S, GB, 8], U32)
        GATE = sb("GATE", [S, 6, GB])
        IDX = sb("IDX", [S, GB, 2])
        ONE1 = sb("ONE1", [S, GB, E])
        ONE2 = sb("ONE2", [S, GB, E])
        COEF = sb("COEF", [S, 2, GB, E])
        COEFT = sb("COEFT", [E, T])
        KM = sb("KM", [128, 2])
        KMEAN = sb("KMEAN", [128, 2])
        RH = sb("RH", [128, 2])
        RL = sb("RL", [128, 6, 2])
        KQ = sb("KQ", [128, 1])

        S_BANK = [psum("S0"), psum("S1")]
        T_BANK = [psum("T0"), psum("T1")]
        O_BANK, M_BANK = psum("OB"), psum("MB")
        A_BANK = [psum("A0"), psum("A1")]

        sem = {name: stack.enter_context(nc.semaphore(name))
               for name in [*GROWS, *CTX_NORM, *ONCE, "x_loaded", "rest_loaded", "w_loaded0", "w_loaded1", "w_loaded2", "w_loaded3",
                            "params_loaded", "consts_set", "stacks_set", "pt_cleared", "consts_copied", "stored", "passed"]}

        def at(name, phase, group=0, more=0):
            return sem[name], count(name, phase, group, more)

        def col(name, k=0):
            c = COLS[name][0] + k
            return COL[:, c:c + 1]

        def row(name):
            return ROW[:, ROWS_BC.index(name), :]

        def tile(name):
            return TILE[:, TILES.index(name), :]

        def att_w(phase, k):
            kind, layer = PHASES[phase]
            at0 = LAYER_AT[layer] + (ATT_COLS if kind == "cross" else 0) + k * D
            return W[:, at0:at0 + D]

        def ff_w(phase, c0, n):
            at0 = LAYER_AT[PHASES[phase][1]] + 2 * ATT_COLS + c0
            return W[:, at0:at0 + n]

        def x_done(phase, group):
            if phase < 0:
                return sem["x_loaded" if isinstance(group, int) and group <= 2 else "rest_loaded"], 16
            return at("x_added" if PHASES[phase][0] in ATT else "y_read", phase, group)

        def letter(phase):
            return {"self": "s", "cross": "q"}.get(PHASES[phase][0], "f")

        def is_cross(phase):
            return PHASES[phase][0] == "cross"

        def nk(phase):
            return S if PHASES[phase][0] == "self" else C

        def masked(phase):
            return PHASES[phase] in (("self", 2), ("self", 3))

        def biased(phase):
            return PHASES[phase] in (("self", 1), ("cross", 1), ("cross", 2))

        def normed_ctx(phase):
            return PHASES[phase] == ("cross", 1)

        block = stack.enter_context(nc.Block())

        @block.sync
        def _(sp):
            sp.dma_start(X[:, 0:2 * GB, :], x[0:2 * GB].rearrange("b s d -> s b d")).then_inc(sem["x_loaded"], 16)
            sp.dma_start(COL[:, :], cols).then_inc(sem["params_loaded"], 16)
            sp.dma_start(ROW[:, :, :], rows).then_inc(sem["params_loaded"], 16)
            sp.dma_start(TILE[:, :, :], tiles).then_inc(sem["params_loaded"], 16)
            for layer in range(4):
                a, z = LAYER_AT[layer], LAYER_AT[layer + 1]
                sp.dma_start(W[:, a:z], weights[:, a:z]).then_inc(sem[f"w_loaded{layer}"], 16)
                if layer == 0:
                    sp.dma_start(X[:, 2 * GB:, :], x[2 * GB:].rearrange("b s d -> s b d")).then_inc(sem["rest_loaded"], 16)
            sp.wait_ge(sem["stacks_set"], 5)

            def stack_parts(done, src, dst, parts, width, hh, par):
                for r, part in enumerate(parts):
                    sp.dma_start(dst[64 * hh + DH * r:64 * hh + DH * (r + 1), par, :, 0:width],
                                 src[64 * hh:64 * hh + 64, part, 0:width]).then_inc(done, 16)

            def attention(st):
                par = st.n0 // GB % 2
                if st.b == 2 and st.has_group(3) and is_cross(st.group(3)[0]):
                    phase, g = st.group(3)
                    wait(sp, *at("cT_psum", phase, g - 1))
                    sp.dma_start(CX[:, 1 - par, :, :], ctx_in[bass.ds(g * GB, GB)].rearrange("b s d -> s b d"))\
                      .then_inc(sem[f"c_loaded{1 - par}"], 16)
                if st.b == 3 and st.has_group(2):
                    (phase, n), (phase2, g2) = st.batch(0), st.group(2)
                    wait_alone(sp, *at("st_psum", phase, 0, 4 * n + 2), sem["passed"])
                    wait_alone(sp, *at("s_psum", phase, 0, 4 * n + 4), sem["passed"])
                    wait(sp, *at("q_low", phase2, g2 + 1))
                    stack_parts(sem["q_stacked0"], QP, QS, Q_PARTS, T, 0, par)
                    wait(sp, *at("k_low", phase2, g2 + 1))
                    stack_parts(sem["k_stacked0"], KP, KS, K_PARTS, GB * nk(phase2), 0, par)
                if st.b == 0 and st.has_group(1):
                    phase, g = st.group(1)
                    wait_alone(sp, *at("st_psum", phase, g - 1), sem["passed"])
                    stack_parts(sem["q_stacked1"], QP, QS, Q_PARTS, T, 1, 1 - par)
                    stack_parts(sem["k_stacked1"], KP, KS, K_PARTS, GB * nk(phase), 1, 1 - par)

            def store(phase):
                def emit(g, par, first, last):
                    wait(sp, *x_done(phase, g + 1))
                    sp.dma_start(out[bass.ds(g * GB, GB)].rearrange("b s d -> s b d") if not isinstance(g, int)
                                 else out[g * GB:(g + 1) * GB].rearrange("b s d -> s b d"),
                                 X[:, bass.ds(g * GB, GB), :] if not isinstance(g, int)
                                 else X[:, g * GB:(g + 1) * GB, :]).then_inc(sem["stored"], 16)
                feed_steps(sp, emit)
                sp.wait_ge(sem["stored"], 16 * NG)

            for phase, (kind, _) in enumerate(PHASES):
                if kind in ATT:
                    attention_steps(sp, attention, phase)
                else:
                    lead_in(attention, phase, 0, 1, 2, 3, 4)
            store(len(PHASES) - 1)

        @block.gpsimd
        def _(pool):
            nc.gpsimd.memset(EPS4[:, :], EPS).then_inc(sem["consts_set"], 1)
            nc.gpsimd.memset(NHALF[:, :], -0.5).then_inc(sem["consts_set"], 1)
            nc.gpsimd.memset(EULER[:, :], 2.718281828459045).then_inc(sem["consts_set"], 1)
            nc.gpsimd.memset(ONES32[:, :, :], 0.0).then_inc(sem["consts_set"], 1)
            pool.wait_ge(sem["consts_set"], 4)
            for r in range(4):
                nc.gpsimd.memset(ONES32[:, r, r * DH:(r + 1) * DH], 1.0).then_inc(sem["consts_set"], 1)
            pool.wait_ge(sem["params_loaded"], 48)
            pool.wait_ge(sem["x_loaded"], 16)

            def rstd(phase, g):
                wait(pool, *at("x_moments", phase, g + 1))
                wait(pool, *at("x_normed", phase, g))
                nc.gpsimd.tensor_tensor(VE[:, :], MV[:, :, 1], EPS4[:, :], ALU.add).then_inc(sem["x_eps"], 1)
                wait(pool, *at("x_eps", phase, g + 1))
                nc.gpsimd.tensor_tensor(RSTD[:, :], VE[:, :], NHALF[:, :], ALU.pow).then_inc(sem["x_rstd"], 1)

            def add_out_bias(phase, g, par, bias):
                wait(pool, *x_done(phase - 1, g + 1))
                if PHASES[phase][0] not in ATT:
                    wait(pool, *x_done(phase, g - 1))
                nc.gpsimd.tensor_tensor(
                    XB[:, par, :, :], X[:, bass.ds(g * GB, GB), :] if not isinstance(g, int) else X[:, g * GB:(g + 1) * GB, :],
                    bias.unsqueeze(1).to_broadcast([S, GB, D]), ALU.add).then_inc(sem["xb_ready"], 1)

            def attention(st):
                par = st.n0 // GB % 2
                if st.has(1):
                    phase, n = st.batch(1)
                    p1 = (st.n0 + 1) % 2
                    wait(pool, *at("max_read", phase, 0, 4 * (n + 1)))
                    wait_alone(pool, *at("mT_psum", phase, 0, n - 1), sem["passed"])
                    negm = NEGM[:, p1, :].rearrange("p (a h) -> p a h", a=2)
                    mr = MR[:, :].rearrange("p (a h) -> p a h", a=2)
                    nc.gpsimd.tensor_copy(MP[:, p1, :, 0, :], negm).then_inc(sem["m_split"], 1)
                    wait(pool, *at("m_split", phase, 0, 3 * n + 1))
                    nc.gpsimd.tensor_tensor(mr, negm, MP[:, p1, :, 0, :], ALU.subtract).then_inc(sem["m_split"], 1)
                    wait_alone(pool, *at("m_split", phase, 0, 3 * n + 2), sem["passed"])
                    nc.gpsimd.tensor_copy(MP[:, p1, :, 1, :], mr).then_inc(sem["m_split"], 1)
                    wait(pool, *at("m_split", phase, 0, 3 * n + 3))
                    nc.gpsimd.tensor_tensor(MP[:, p1, :, 2, :], mr, MP[:, p1, :, 1, :], ALU.subtract)\
                      .then_inc(sem["m_parts"], 1)
                if st.b == 2 and st.has_group(3):
                    rstd(*st.group(3))
                if st.b == 0 and st.has_group(2):
                    phase, g = st.group(2)
                    if normed_ctx(phase):
                        pool.wait_ge(sem["c_moments"], GB * (g + 1))
                        wait(pool, sem["c_normed"], GB * g)
                        nc.gpsimd.tensor_tensor(CVE[:, :], CMV[:, :, 1], EPS4[0:C, :], ALU.add).then_inc(sem["c_eps"], 1)
                        pool.wait_ge(sem["c_eps"], g + 1)
                        nc.gpsimd.tensor_tensor(CRSTD[:, :], CVE[:, :], NHALF[0:C, :], ALU.pow).then_inc(sem["c_rstd"], 1)
                if st.feeds(B - 3):
                    rstd(st.phase + 1, 0)
                if st.feeds(B) and PHASES[st.phase + 1][0] == "moe":
                    gates(st.phase + 1, 0)
                if st.b == 2 and st.has_group(2):
                    phase, g = st.group(2)
                    for f, p, w, c in ((QF, QP, T, "q"), (KF, KP, GB * nk(phase), "k")):
                        wait(pool, *at(f"{c}_copied", phase, g + 1))
                        nc.gpsimd.tensor_tensor(f[:, 0:w], f[:, 0:w], p[:, 0, 0:w], ALU.subtract)\
                          .then_inc(sem[f"{c}_resid"], 1)
                if st.b == 3 and st.has_group(2):
                    phase, g = st.group(2)
                    for f, p, w, c in ((QF, QP, T, "q"), (KF, KP, GB * nk(phase), "k")):
                        wait(pool, *at(f"{c}_mid", phase, g + 1))
                        nc.gpsimd.tensor_tensor(p[:, 2, 0:w], f[:, 0:w], p[:, 1, 0:w], ALU.subtract)\
                          .then_inc(sem[f"{c}_low"], 1)
                if st.phase and not st.n0 and st.i is None:
                    wait(pool, *x_done(st.phase - 1, NG))
                if st.b == 1 and st.has_group(0):
                    phase, g = st.group(0)
                    add_out_bias(phase, g, par, row(f"bo{PHASES[phase][1]}{letter(phase)}"))

            def gates(phase, g):
                wait(pool, *at("top_diff", phase, g + 1))
                wait(pool, *at("gate_steps", phase, g))
                nc.gpsimd.tensor_tensor(GATE[:, 1, :], EULER[:, :], GATE[:, 0, :], ALU.pow).then_inc(sem["top_exp"], 1)

            def feed(phase):
                kind, layer = PHASES[phase]
                wait(pool, *x_done(phase - 1, NG))

                def emit(g, par, first, last):
                    if not last:
                        rstd(phase, g + 1)
                    if kind != "moe":
                        add_out_bias(phase, g, par, row(f"f{layer}"))
                    elif not last:
                        gates(phase, g + 1)
                    if last:
                        lead_in(attention, phase, 0, 1, 2, 3, 4)
                feed_steps(pool, emit)

            for phase, (kind, _) in enumerate(PHASES):
                if kind in ATT:
                    attention_steps(pool, attention, phase)
                else:
                    feed(phase)

        @block.vector
        def _(dve):
            nc.vector.memset(V32[:, :, :, :, :], 0.0).then_inc(sem["stacks_set"], 1)
            for par in range(2):
                nc.vector.memset(KS[:, par, :, :], 1.0).then_inc(sem["stacks_set"], 1)
                nc.vector.memset(QS[:, par, :, :], 0.0).then_inc(sem["stacks_set"], 1)
            dve.wait_ge(sem["params_loaded"], 48)
            dve.wait_ge(sem["x_loaded"], 16)
            dve.wait_ge(sem["consts_set"], 8)
            nc.vector.tensor_copy(IDENT_B[:, :], tile("ident")).then_inc(sem["consts_copied"], 1)
            nc.vector.tensor_copy(MASK[:, 0, :], tile("causal")).then_inc(sem["consts_copied"], 1)
            nc.vector.tensor_copy(MASK[:, 1, :], tile("causalT")).then_inc(sem["consts_copied"], 1)

            def xs(g, b=None):
                if b is None:
                    return X[:, g * GB:(g + 1) * GB, :] if isinstance(g, int) else X[:, bass.ds(g * GB, GB), :]
                n = g * GB + b
                return X[:, n:n + 1, :] if isinstance(n, int) else X[:, bass.ds(n, 1), :]

            def moments(phase, g):
                wait(dve, *x_done(phase - 1, g + 1))
                wait(dve, *at("x_rstd", phase, g))
                for b in range(GB):
                    nc.vector.bn_stats(ST[:, b, :], xs(g, b)).then_inc(sem["x_stats"], 1)
                for b in range(GB):
                    wait_alone(dve, *at("x_stats", phase, g, b + 1), sem["passed"])
                    nc.vector.bn_aggr(MV[:, b, :], ST[:, b, :]).then_inc(sem["x_moments"], 1)

            def normalise(phase, g):
                wait(dve, *at("x_rstd", phase, g + 1))
                wait(dve, *at("xT_psum", phase, g))
                for b in range(GB):
                    nc.vector.tensor_scalar(XN[:, b:b + 1, :], xs(g, b), MV[:, b, 0:1], RSTD[:, b:b + 1],
                                            ALU.subtract, ALU.mult).then_inc(sem["x_normed"], 1)

            def ctx_moments(phase, g, pair, par):
                dve.wait_ge(*at(f"c_loaded{par}", phase, 0, 16 * (pair + 1)))
                wait(dve, sem["c_rstd"], g)
                for b in range(GB):
                    nc.vector.bn_stats(CST[:, b, :], CX[:, par, b, :]).then_inc(sem["c_stats"], 1)
                for b in range(GB):
                    wait_alone(dve, sem["c_stats"], GB * g + b + 1, sem["passed"])
                    nc.vector.bn_aggr(CMV[:, b, :], CST[:, b, :]).then_inc(sem["c_moments"], 1)

            def v_columns(keys, par):
                return bass.AP(tensor=V32[:, :, :, :, :].tensor, offset=par * GB * H * 4 * DH,
                               ap=[[2 * GB * H * 4 * DH, keys], [16 * DH, GB * H // 4], [5 * DH, 4], [1, DH]])

            def block_router(phase):
                n = [0]

                def done(ins):
                    n[0] += 1
                    ins.then_inc(sem["mask_steps"], 1)
                    dve.wait_ge(sem["mask_steps"], n[0])

                dve.wait_ge(*at("k_psum", phase, 1))
                done(nc.vector.tensor_reduce(KM[:, :], A_BANK[0][:, 0:S].rearrange("p (a t) -> p a t", a=2), AX.X, ALU.add))
                done(nc.vector.tensor_scalar(KMEAN[:, :], KM[:, :], 1.0 / 64, None, ALU.mult))
                dve.wait_ge(sem["mask_psum"], 2)
                done(nc.vector.tensor_scalar(RL[:, 0, :], A_BANK[0][:, 0:2], col("r2"), None, ALU.add))
                dve.wait_ge(sem["mask_exp"], 1)
                done(nc.vector.tensor_scalar(RL[:, 2, :], RL[:, 1, :], 1.0, None, ALU.add))
                done(nc.vector.reciprocal(RL[:, 3, :], RL[:, 2, :]))
                done(nc.vector.tensor_scalar(RL[:, 4, :], RL[:, 3, :], 0.5, None, ALU.is_gt))
                done(nc.vector.tensor_copy(KQ[0:64, :], RL[0:64, 4, 0:1]))
                done(nc.vector.tensor_copy(KQ[64:128, :], RL[64:128, 4, 1:2]))
                done(nc.vector.tensor_scalar(RL[:, 5, :], RL[:, 4, :], KQ[:, 0:1], None, ALU.mult))
                done(nc.vector.tensor_scalar(RL[:, 2, :], RL[:, 5, :], 1.0, -HIDE, ALU.subtract, ALU.mult))
                for m, name in ((2, "causal"), (3, "causalT")):
                    for j in range(2):
                        done(nc.vector.tensor_scalar(MASK[:, m, 64 * j:64 * j + 64], tile(name)[:, 64 * j:64 * j + 64],
                                                     RL[:, 2, j:j + 1], None, ALU.add))

            def route(phase, g, par):
                wait(dve, *at("lg_psum", phase, g + 1))
                rb = COL[:, COLS["router"][0]:COLS["router"][0] + E].unsqueeze(1).to_broadcast([S, GB, E])
                nc.vector.tensor_tensor(LG[:, :, :], A_BANK[1][:, 0:GB * E].rearrange("p (b e) -> p b e", b=GB), rb, ALU.add)\
                  .then_inc(sem["lg_ready"], 1)
                wait_alone(dve, *at("lg_ready", phase, g + 1), sem["passed"])
                for b in range(GB):
                    nc.vector.max(TOPV[:, b, :], LG[:, b, :]).then_inc(sem["top_vals"], 1)
                for b in range(GB):
                    wait_alone(dve, *at("top_vals", phase, g, b + 1), sem["passed"])
                    nc.vector.max_index(TOPI[:, b, :], TOPV[:, b, :], LG[:, b, :]).then_inc(sem["top_idx"], 1)
                wait(dve, *at("top_exp", phase, g))
                nc.vector.tensor_tensor(GATE[:, 0, :], TOPV[:, :, 1], TOPV[:, :, 0], ALU.subtract).then_inc(sem["top_diff"], 1)
                wait(dve, *at("top_idx", phase, g + 1))
                nc.vector.tensor_copy(IDX[:, :, :], TOPI[:, :, 0:2]).then_inc(sem["gate_steps"], 1)
                wait(dve, *at("top_exp", phase, g + 1))
                nc.vector.tensor_scalar(GATE[:, 2, :], GATE[:, 1, :], 1.0, None, ALU.add).then_inc(sem["gate_steps"], 1)
                wait(dve, *at("gate_steps", phase, g, 2))
                nc.vector.reciprocal(GATE[:, 3, :], GATE[:, 2, :]).then_inc(sem["gate_steps"], 1)
                wait(dve, *at("gate_steps", phase, g, 3))
                nc.vector.tensor_tensor(GATE[:, 4, :], GATE[:, 1, :], GATE[:, 3, :], ALU.mult).then_inc(sem["gate_steps"], 1)
                wait(dve, *at("gate_steps", phase, g, 4))
                iota = COL[:, COLS["iota"][0]:COLS["iota"][0] + E]
                for b in range(GB):
                    nc.vector.tensor_scalar(ONE1[:, b, :], iota, IDX[:, b, 0:1], GATE[:, 3, b:b + 1],
                                            ALU.is_equal, ALU.mult).then_inc(sem["coef_one"], 1)
                    nc.vector.tensor_scalar(ONE2[:, b, :], iota, IDX[:, b, 1:2], GATE[:, 4, b:b + 1],
                                            ALU.is_equal, ALU.mult).then_inc(sem["coef_one"], 1)
                wait(dve, *at("coef_one", phase, g + 1))
                nc.vector.tensor_tensor(COEF[:, par, :, :], ONE1[:, :, :], ONE2[:, :, :], ALU.add)\
                  .then_inc(sem["coef_ready"], 1)

            def route_sum(phase, g, par):
                wait(dve, *at("coefT_psum", phase, g + 1))
                nc.vector.tensor_copy(COEFT[:, :], A_BANK[1][0:E, :]).then_inc(sem["coefT_ready"], 1)
                wait(dve, *at("b2_psum", phase, g + 1))
                nc.vector.tensor_tensor(XB[:, par, :, :], A_BANK[1][:, :].rearrange("p (b d) -> p b d", b=GB), xs(g), ALU.add)\
                  .then_inc(sem["acc_ready"], 1)

            def attention(st):
                par = st.n0 // GB % 2

                def row_max(u):
                    phase, n = st.batch(2)
                    keys, p2 = nk(phase), st.n0 % 2
                    if u == 0:
                        wait(dve, *at("m_parts", phase, 0, n - 1))
                    wait(dve, *at("s_psum", phase, 0, 4 * n + u + 1))
                    nc.vector.tensor_reduce(NEGM[:, p2, 4 * u:4 * u + 4],
                                            S_BANK[u % 2][:, 0:4 * keys].rearrange("p (h k) -> p h k", h=4),
                                            AX.X, ALU.max, negate=True).then_inc(sem["max_read"], 1)

                if st.has(2):
                    row_max(0)
                if st.has(2):
                    row_max(1)
                if st.has(1):
                    phase, n = st.batch(1)
                    p1 = (st.n0 + 1) % 2
                    wait(dve, *at("mT_psum", phase, 0, n + 1))
                    phase, pairs = st.pairs(1)
                    for hh in range(2):
                        wait(dve, *at(f"m_stacked{p1}{hh}", phase, 0, 16 * pairs))
                    nc.vector.tensor_copy(MT[:, p1, :], M_BANK[0:2 * MROWS * HH, 0:S // 2].bitcast(BF16))\
                      .then_inc(sem["mT_ready"], 1)
                if st.b == 0 and st.has_group(2):
                    phase, g = st.group(2)
                    if normed_ctx(phase):
                        ctx_moments(phase, g, st.ctx_pair(), par)
                if st.b == 2 and st.has_group(3):
                    moments(*st.group(3))
                if st.b == 3 and st.has_group(2):
                    phase, g = st.group(2)
                    keys = nk(phase)
                    for f, p, w, c in ((QF, QP, T, "q"), (KF, KP, GB * keys, "k")):
                        wait(dve, *at(f"{c}_resid", phase, g + 1))
                        nc.vector.tensor_copy(p[:, 1, 0:w], f[:, 0:w]).then_inc(sem[f"{c}_mid"], 1)
                if st.has(-1):
                    phase, n = st.batch(-1)
                    wait(dve, *at("sums_done", phase, 0, n + 1))
                    nc.vector.reciprocal(REC[:, :], O_BANK[:, 0:S]).then_inc(sem["rec_ready"], 1)
                if st.feeds(B - 3):
                    moments(st.phase + 1, 0)
                if st.feeds(B - 2):
                    normalise(st.phase + 1, 0)
                if st.b == 1 and st.has_group(2):
                    normalise(*st.group(2))
                if st.has(-1):
                    phase, n = st.batch(-1)
                    wait(dve, *at("pv_done", phase, 0, n + 1))
                    wait(dve, *at("rec_ready", phase, 0, n + 1))
                    nc.vector.tensor_tensor(AT[:, :], M_BANK[:, S:2 * S], REC[:, :], ALU.mult).then_inc(sem["att_ready"], 1)
                if st.i is None and st.chained and st.n0 >= B - 1:
                    nc.vector.memset(PT[64:128, (st.n0 + 1) % 2, :, :], 0.0).then_inc(sem["pt_cleared"], 1)
                if st.routes_blocks():
                    block_router(st.phase)
                if st.has(2):
                    row_max(2)
                    row_max(3)
                if st.has(-1):
                    phase, n = st.batch(-1)
                    gp, bp = (st.n0 - 1) // GB % 2, (st.n0 - 1) % GB
                    wait(dve, *at("o_psum", phase, 0, n + 1))
                    phase, g = st.group(0 if st.b else -1)
                    wait(dve, *at("xb_ready", phase, g + 1))
                    dst = X[:, n:n + 1, :] if isinstance(n, int) else X[:, bass.ds(n, 1), :]
                    nc.vector.tensor_tensor(dst, O_BANK[:, 0:D].unsqueeze(1), XB[:, gp, bp:bp + 1, :], ALU.add)\
                      .then_inc(sem["x_added"], 1)
                if st.b == 1 and st.has_group(2) and normed_ctx(st.group(2)[0]):
                    _, g = st.group(2)
                    dve.wait_ge(sem["c_rstd"], g + 1)
                    for b in range(GB):
                        nc.vector.tensor_scalar(CX[:, par, b, :], CX[:, par, b, :], CMV[:, b, 0:1], CRSTD[:, b:b + 1],
                                                ALU.subtract, ALU.mult).then_inc(sem["c_normed"], 1)
                if st.b == 0 and st.has_group(1):
                    phase, g = st.group(1)
                    keys = nk(phase)
                    wait(dve, *at("v_psum", phase, g + 1))
                    wait(dve, *at("pv_done", phase, g - 1))
                    vb = A_BANK[0 if is_cross(phase) else 1][0:keys, :].rearrange("p (c r e) -> p c r e", r=4, e=DH)
                    v32 = v_columns(keys, 1 - par)
                    if biased(phase):
                        bias = row(f"bv{PHASES[phase][1]}{letter(phase)}")[0:keys, :]\
                            .rearrange("p (c r e) -> p c r e", r=4, e=DH)
                        for b in range(GB):
                            nc.vector.tensor_tensor(v32[:, 4 * b:4 * b + 4], vb[:, 4 * b:4 * b + 4], bias, ALU.add)\
                              .then_inc(sem["v_ready"], 1)
                    else:
                        for b in range(0, GB, 2):
                            nc.vector.tensor_copy(v32[:, 4 * b:4 * b + 8], vb[:, 4 * b:4 * b + 8])\
                              .then_inc(sem["v_ready"], 2)
                if st.feeds(B) and PHASES[st.phase + 1][0] == "moe":
                    route(st.phase + 1, 0, 0)
                    route_sum(st.phase + 1, 0, 0)

            def feed(phase):
                kind, layer = PHASES[phase]
                def mix(g, e, par):
                    wait(dve, *at("y_psum", phase, g, e + 1))
                    wait(dve, *at("acc_ready", phase, g + 1))
                    bank = (O_BANK, M_BANK)[e % 2]
                    for b in range(GB):
                        if e:
                            wait(dve, *at("y_read", phase, g, GB * (e - 1) + b + 1))
                        nc.vector.scalar_tensor_tensor(
                            xs(g, b) if e == E - 1 else XB[:, par, b:b + 1, :],
                            bank[:, b * D:(b + 1) * D].unsqueeze(1), COEF[:, par, b, e:e + 1], XB[:, par, b:b + 1, :],
                            ALU.mult, ALU.add).then_inc(sem["y_read"], 1)

                def emit_moe(g, par, first, last):
                    for e in range(E):
                        if e == 1 and not last:
                            moments(phase, g + 1)
                        if e == 2 and not last:
                            normalise(phase, g + 1)
                        if e == 4 and not last:
                            route(phase, g + 1, 1 - par)
                        if e == 6 and not last:
                            route_sum(phase, g + 1, 1 - par)
                        if last and 1 <= e <= len(LEAD_IN):
                            lead_in(attention, phase, e - 1)
                        if e:
                            mix(g, e - 1, par)
                        elif not first:
                            mix(g - 1, E - 1, 1 - par)
                    if last:
                        mix(g, E - 1, par)

                def finish(g, par):
                    wait(dve, *at("y_psum", phase, g + 1))
                    wait(dve, *at("xb_ready", phase, g + 1))
                    nc.vector.tensor_tensor(xs(g), (O_BANK, M_BANK)[par][:, :].rearrange("p (b d) -> p b d", b=GB),
                                            XB[:, par, :, :], ALU.add).then_inc(sem["y_read"], 1)

                def emit(g, par, first, last):
                    if last:
                        lead_in(attention, phase, 0, 1)
                    if kind == "geglu":
                        wait(dve, *at("y_psum", phase, g - 1))
                        if first:
                            wait(dve, *at("pv_done", phase))
                        for c in range(NC):
                            wait(dve, *at("fc1_psum", phase, g, c + 1))
                            wait(dve, *at("gate_done", phase, g, c + 1))
                            nc.vector.scalar_tensor_tensor(
                                PT[:, par, 4 * c:4 * c + 4, :].rearrange("p h s -> p (h s)"), S_BANK[c % 2][:, :], col("h0", c),
                                GL[:, c % 2, :], ALU.add, ALU.mult).then_inc(sem["hid_done"], 1)
                            if c == 0 and not last:
                                moments(phase, g + 1)
                            if c == 2 and not last:
                                normalise(phase, g + 1)
                    elif not last:
                        moments(phase, g + 1)
                        normalise(phase, g + 1)
                    if last:
                        lead_in(attention, phase, 2)
                    if not first:
                        finish(g - 1, 1 - par)
                    if last:
                        lead_in(attention, phase, 3)
                        finish(g, par)
                        lead_in(attention, phase, 4)

                feed_steps(dve, emit_moe if kind == "moe" else emit)

            for phase, (kind, _) in enumerate(PHASES):
                if kind in ATT:
                    attention_steps(dve, attention, phase)
                else:
                    feed(phase)

        @block.scalar
        def _(act):
            act.wait_ge(sem["params_loaded"], 48)

            def turned(phase, g, par):
                k = f"{PHASES[phase][1]}{letter(phase)}"
                wait(act, *at("xT_psum", phase, g + 1))
                if PHASES[phase][0] in ATT:
                    wait(act, *at("v_psum", phase, g - 1))
                else:
                    wait(act, *at("y_psum", phase, g - 1))
                nc.scalar.activation(XT[:, par, :], A_BANK[0][:, :], ACT.Identity, bias=col("b" + k), scale=col("g" + k))\
                  .then_inc(sem["xT_ready"], 1)

            def attention(st):
                par = st.n0 // GB % 2

                def stack_maxima():
                    phase, n = st.batch(1)
                    p1 = (st.n0 + 1) % 2
                    g1, b1 = (st.n0 + 1) // GB, (st.n0 + 1) % GB
                    wait(act, *at("mT_ready", phase, 0, n + 1))
                    for hh in range(2):
                        act.dma_start(QS[64 * hh + ROWS:64 * hh + ROWS + MROWS, g1 % 2, :, b1 * S:(b1 + 1) * S],
                                     MT[hh * MROWS * HH:(hh + 1) * MROWS * HH, p1, :])\
                          .then_inc(sem[f"m_stacked{p1}{hh}"], 16)

                def exps(u):
                    phase, n = st.batch(0)
                    keys = nk(phase)
                    scale = (SCALE_CROSS if is_cross(phase) else SCALE_SELF)[PHASES[phase][1]]
                    if u == 0:
                        wait(act, *at("pv_done", phase, 0, n - 1))
                        if is_cross(phase):
                            act.wait_ge(sem["pt_cleared"], 2 * PHASES[phase][1] + 1 + (st.n0 % B > 0))
                    wait(act, *at("st_psum", phase, 0, 4 * n + u + 1))
                    nc.scalar.activation(PT[0:keys, st.n0 % 2, 4 * u:4 * u + 4, :].rearrange("p h s -> p (h s)"),
                                         T_BANK[u % 2][0:keys, :], ACT.Exp, scale=scale).then_inc(sem["exp_done"], 1)

                if st.has(0):
                    exps(0)
                    exps(1)
                if st.b == 2 and st.has_group(2):
                    phase, g = st.group(2)
                    cross = is_cross(phase)
                    if cross:
                        wait(act, *at("cT_psum", phase, g + 1))
                        if normed_ctx(phase):
                            nc.scalar.activation(CXT[:, par, :], A_BANK[1][:, 0:CT], ACT.Identity,
                                                 bias=col("b1c"), scale=col("g1c")).then_inc(sem["cT_ready"], 1)
                        else:
                            nc.scalar.activation(CXT[:, par, :], A_BANK[1][:, 0:CT], ACT.Copy).then_inc(sem["cT_ready"], 1)
                    for f, p, w, c, bank in ((QF, QP, T, "q", A_BANK[0 if cross else 1]),
                                             (KF, KP, GB * nk(phase), "k", A_BANK[1 if cross else 0])):
                        if c == "k" and st.has(1):
                            stack_maxima()
                        wait(act, *at(f"{c}_psum", phase, g + 1))
                        wait(act, *at(f"{c}_low", phase, g))
                        wait(act, *at(f"{c}_stacked1", phase, g))
                        if c == "k" and st.routes_blocks():
                            act.wait_ge(sem["mask_steps"], 1)
                        bias = col(f"b{c}{PHASES[phase][1]}{letter(phase)}") if biased(phase) else 0.0
                        nc.scalar.activation(f[:, 0:w], bank[:, 0:w], ACT.Identity, bias=bias).then_inc(sem[f"{c}_copied"], 1)
                        nc.scalar.activation(p[:, 0, 0:w], bank[:, 0:w], ACT.Identity, bias=bias).then_inc(sem[f"{c}_copied"], 1)
                    if st.routes_blocks():
                        act.wait_ge(sem["mask_psum"], 1)
                        nc.scalar.activation(RH[:, :], A_BANK[0][:, 0:2], ACT.Relu, bias=col("r1")).then_inc(sem["mask_relu"], 1)
                        act.wait_ge(sem["mask_steps"], 3)
                        nc.scalar.activation(RL[:, 1, :], RL[:, 0, :], ACT.Exp, scale=-1.0).then_inc(sem["mask_exp"], 1)
                if st.has(1) and not (st.b == 2 and st.has_group(2)):
                    stack_maxima()
                if st.has(0):
                    exps(2)
                    exps(3)
                if st.b == 1 and st.has_group(2):
                    phase, g = st.group(2)
                    turned(phase, g, par)
                if st.feeds(B - 2):
                    turned(st.phase + 1, 0, 0)

            def feed(phase):
                kind, layer = PHASES[phase]
                func = {"geglu": ACT.Gelu_apprx_sigmoid, "moe": ACT.Gelu}.get(kind, ACT.Relu if layer == 2 else ACT.Gelu)
                wait(act, *at("pv_done", phase))

                def hidden(g, e, par):
                    unit = e if kind == "moe" else 0
                    up = e % 2 if kind == "moe" else par
                    wait(act, *at("y_psum", phase, g, unit - 1))
                    for c in range(NC):
                        wait(act, *at("fc1_psum", phase, g, NC * unit + c + 1))
                        nc.scalar.activation(PT[:, up, 4 * c:4 * c + 4, :].rearrange("p h s -> p (h s)"),
                                             (T_BANK[0], S_BANK[0], T_BANK[1], S_BANK[1])[c][:, :], func,
                                             bias=col(f"h{layer}", NC * e + c)).then_inc(sem["hid_done"], 1)

                def emit(g, par, first, last):
                    if kind == "geglu":
                        for c in range(NC):
                            wait(act, *at("gate_psum", phase, g, c + 1))
                            wait(act, *at("hid_done", phase, g, c - 1))
                            nc.scalar.activation(GL[:, c % 2, :], T_BANK[c % 2][:, :], func, bias=col("h0", NC + c))\
                              .then_inc(sem["gate_done"], 1)
                    elif kind == "ffn":
                        hidden(g, 0, par)
                    else:
                        for e in range(E):
                            hidden(g, e, par)
                            if e == 2 and not last:
                                turned(phase, g + 1, 1 - par)
                            if last and 1 <= e <= len(LEAD_IN):
                                lead_in(attention, phase, e - 1)
                    if kind != "moe" and not last:
                        turned(phase, g + 1, 1 - par)
                    if kind != "moe" and last:
                        lead_in(attention, phase, 0, 1, 2, 3, 4)

                feed_steps(act, emit)

            for phase, (kind, _) in enumerate(PHASES):
                if kind in ATT:
                    attention_steps(act, attention, phase)
                else:
                    feed(phase)

        @block.tensor
        def _(pe):
            pe.wait_ge(sem["params_loaded"], 48)
            pe.wait_ge(sem["consts_copied"], 3)
            for name in FIRST:
                pe.sem_inc(sem[name], FIRST[name])
            pe.wait_ge(sem["w_loaded0"], 16)
            ident = tile("ident")

            def turn(phase, g):
                wait(pe, *at("x_normed", phase, g + 1))
                for b in range(GB):
                    last = nc.tensor.transpose(A_BANK[0][:, b * S:(b + 1) * S], XN[:, b, :], ident)
                last.then_inc(sem["xT_psum"], 1)

            ff_router = COL[:, COLS["router_w"][0]:COLS["router_w"][0] + E]

            def route(phase, g, par):
                wait(pe, *at("xT_ready", phase, g + 1))
                wait(pe, *at("acc_ready", phase, g))
                for b in range(GB):
                    last = nc.tensor.matmul(A_BANK[1][:, b * E:(b + 1) * E], XT[:, par, b * S:(b + 1) * S],
                                            ff_router, start=True, stop=True, skip_group_check=True)
                last.then_inc(sem["lg_psum"], 1)

            def route_turn(phase, g, par):
                wait(pe, *at("coef_ready", phase, g + 1))
                for b in range(GB):
                    last = nc.tensor.transpose(A_BANK[1][0:E, b * S:(b + 1) * S], COEF[:, par, b, :], ident)
                last.then_inc(sem["coefT_psum"], 1)

            def route_bias(phase, g):
                wait(pe, *at("coefT_ready", phase, g + 1))
                for b in range(GB):
                    last = nc.tensor.matmul(A_BANK[1][:, b * D:(b + 1) * D], COEFT[:, b * S:(b + 1) * S], tile("b2")[0:E, :],
                                            start=True, stop=True, skip_group_check=True)
                last.then_inc(sem["b2_psum"], 1)

            def attention(st):
                par = st.n0 // GB % 2

                def mask(phase, bank, turned):
                    m = (2 if PHASES[phase][1] == 2 else 0) + turned
                    nc.tensor.matmul(bank[:, :].rearrange("p (h k) -> p h k", h=4), IDENT_B[:, :],
                                     MASK[:, m, :].unsqueeze(1).to_broadcast([S, 4, S]),
                                     start=True, stop=False, skip_group_check=True)

                def scores(u):
                    phase, n = st.batch(2)
                    keys = nk(phase)
                    hh, h0 = u // 2, 4 * (u % 2)
                    g2, b2 = (st.n0 + 2) // GB % 2, (st.n0 + 2) % GB
                    if u % 2 == 0 and b2 == 0:
                        _, g = st.group(1)
                        wait(pe, *at(f"q_stacked{hh}", phase, g + 1))
                        wait(pe, *at(f"k_stacked{hh}", phase, g + 1))
                    wait(pe, *at("max_read", phase, 0, 4 * n + u - 1))
                    bank = S_BANK[u % 2]
                    if masked(phase):
                        mask(phase, bank, False)
                    for j in range(4):
                        last = nc.tensor.matmul(bank[:, j * keys:(j + 1) * keys],
                                                QS[64 * hh:64 * hh + ROWS, g2, h0 + j, b2 * S:(b2 + 1) * S],
                                                KS[64 * hh:64 * hh + ROWS, g2, h0 + j, b2 * keys:(b2 + 1) * keys],
                                                start=not masked(phase), stop=True, skip_group_check=True)
                    last.then_inc(sem["s_psum"], 1)

                def scores_t(u):
                    phase, n = st.batch(0)
                    keys = nk(phase)
                    hh, h0 = u // 2, 4 * (u % 2)
                    if u % 2 == 0:
                        wait(pe, *at(f"m_stacked{st.n0 % 2}{hh}", phase, 0, 16 * (st.pairs(0)[1] + 1)))
                    wait(pe, *at("exp_done", phase, 0, 4 * n + u - 1))
                    bank = T_BANK[u % 2]
                    if masked(phase):
                        mask(phase, bank, True)
                    for j in range(4):
                        last = nc.tensor.matmul(bank[0:keys, j * S:(j + 1) * S],
                                                KS[64 * hh:64 * hh + 64, par, h0 + j, st.b * keys:(st.b + 1) * keys],
                                                QS[64 * hh:64 * hh + 64, par, h0 + j, st.b * S:(st.b + 1) * S],
                                                start=not masked(phase), stop=True, skip_group_check=True)
                    last.then_inc(sem["st_psum"], 1)

                if st.i is None and PHASES[st.phase] == ("self", 2) and st.n0 == -2:
                    pe.wait_ge(sem["mask_steps"], 14)
                for u in range(2):
                    if st.has(0):
                        scores_t(u)
                    if st.has(2):
                        scores(u)
                if st.b == 2 and st.has_group(2):
                    phase, g = st.group(2)
                    if is_cross(phase):
                        if normed_ctx(phase):
                            pe.wait_ge(sem["c_normed"], GB * (g + 1))
                        else:
                            pe.wait_ge(*at(f"c_loaded{par}", phase, 0, (st.ctx_pair() + 1) * 16))
                        for b in range(GB):
                            last = nc.tensor.transpose(A_BANK[1][:, b * C:(b + 1) * C], CX[:, par, b, :], ident[0:C, 0:C])
                        last.then_inc(sem["cT_psum"], 1)
                if st.b == 2 and st.has_group(2):
                    phase, g = st.group(2)
                    cross = is_cross(phase)
                    wait(pe, *at("xT_ready", phase, g + 1))
                    nc.tensor.matmul(A_BANK[0 if cross else 1][:, :], att_w(phase, 0), XT[:, par, :],
                                     start=True, stop=True).then_inc(sem["q_psum"], 1)
                if st.feeds(B) and PHASES[st.phase + 1][0] == "moe":
                    route(st.phase + 1, 0, 0)
                def turn_maxima():
                    phase, n = st.batch(1)
                    wait_alone(pe, *at("m_parts", phase, 0, n + 1), sem["passed"])
                    if st.n0 == -1 and st.phase:
                        wait_alone(pe, *x_done(st.phase - 1, NG), sem["passed"])
                    nc.tensor.transpose(M_BANK[0:2 * MROWS * HH, 0:S // 2].bitcast(BF16),
                                        MP[:, (st.n0 + 1) % 2, :, :, :].rearrange("p a m h -> p (a m h)"), IDENT_B[:, :])\
                      .then_inc(sem["mT_psum"], 1)

                def probs_times(products):
                    gp, bp = (st.n0 - 1) // GB % 2, (st.n0 - 1) % GB
                    for r in range(4):
                        if r == 2 and not products and st.has(1):
                            turn_maxima()
                        for j in range(4):
                            h = 4 * j + r
                            left = V32[:, gp, bp, h, :] if products else ONES32[:, r, :]
                            bank = M_BANK[:, S:2 * S] if products else O_BANK[:, 0:S]
                            last = nc.tensor.matmul(bank[4 * DH * j:4 * DH * (j + 1), :], left,
                                                    PT[:, (st.n0 - 1) % 2, h, :],
                                                    start=r == 0, stop=r == 3, skip_group_check=True)
                    last.then_inc(sem["pv_done" if products else "sums_done"], 1)

                if st.has(-1):
                    phase, n = st.batch(-1)
                    wait(pe, *at("exp_done", phase, 0, 4 * (n + 1)))
                    wait(pe, *at("x_added", phase, 0, n))
                    probs_times(False)
                elif st.has(1):
                    turn_maxima()
                if st.has(-1):
                    phase, g = st.group(0 if st.b else -1)
                    wait(pe, *at("v_ready", phase, g + 1))
                    wait(pe, *(at("mT_ready", st.batch(1)[0], 0, st.batch(1)[1] + 1) if st.has(1) else at("mT_ready", st.phase, NG)))
                    probs_times(True)
                if st.b == 2 and st.has_group(2):
                    phase, g = st.group(2)
                    cross = is_cross(phase)
                    if cross:
                        wait(pe, *at("cT_ready", phase, g + 1))
                    src = CXT[:, par, :] if cross else XT[:, par, :]
                    nc.tensor.matmul(A_BANK[1 if cross else 0][:, 0:GB * nk(phase)], att_w(phase, 1), src,
                                     start=True, stop=True).then_inc(sem["k_psum"], 1)
                    if st.routes_blocks():
                        wait(pe, *at("k_copied", phase, g + 1))
                        pe.wait_ge(sem["mask_steps"], 2)
                        nc.tensor.matmul(A_BANK[0][:, 0:2], tile("rw1"), KMEAN[:, :], start=True, stop=True)\
                          .then_inc(sem["mask_psum"], 1)
                        pe.wait_ge(sem["mask_relu"], 1)
                        nc.tensor.matmul(A_BANK[0][:, 0:2], tile("rw2"), RH[:, :], start=True, stop=True)\
                          .then_inc(sem["mask_psum"], 1)
                        pe.wait_ge(sem["mask_steps"], 3)
                if st.b == 0 and st.has_group(1):
                    phase, g = st.group(1)
                    cross, keys = is_cross(phase), nk(phase)
                    wait(pe, *at("q_copied", phase, g + 1))
                    src = CXT if cross else XT
                    for b in range(GB):
                        last = nc.tensor.matmul(A_BANK[0 if cross else 1][0:keys, b * D:(b + 1) * D],
                                                src[:, 1 - par, b * keys:(b + 1) * keys], att_w(phase, 2),
                                                start=True, stop=True, skip_group_check=True)
                    last.then_inc(sem["v_psum"], 1)
                for u in (2, 3):
                    if st.has(0):
                        scores_t(u)
                    if st.has(2):
                        scores(u)
                if st.feeds(B - 2):
                    wait(pe, *at("v_ready", st.phase, NG))
                    turn(st.phase + 1, 0)
                if st.has(-1):
                    phase, n = st.batch(-1)
                    wait(pe, *at("att_ready", phase, 0, n + 1))
                    nc.tensor.matmul(O_BANK[:, 0:D], AT[:, :], att_w(phase, 3), start=True, stop=True)\
                      .then_inc(sem["o_psum"], 1)
                if st.b == 1 and st.has_group(2):
                    phase, g = st.group(2)
                    wait(pe, *at("v_ready", phase, g))
                    wait(pe, *at("k_copied", phase, g))
                    turn(phase, g)
                if st.feeds(B) and PHASES[st.phase + 1][0] == "moe":
                    route_turn(st.phase + 1, 0, 0)
                    route_bias(st.phase + 1, 0)

            def feed(phase):
                kind, layer = PHASES[phase]

                def fc1(g, e, par):
                    unit = e if kind == "moe" else 0
                    wait(pe, *at("xT_ready", phase, g + 1))
                    for c in range(NC):
                        if kind == "geglu":
                            wait(pe, *at("gate_done", phase, g, c - 1))
                            nc.tensor.matmul(T_BANK[c % 2][:, :], ff_w(phase, F + c * 128, 128), XT[:, par, :],
                                             start=True, stop=True).then_inc(sem["gate_psum"], 1)
                            wait(pe, *at("hid_done", phase, g, c - 1))
                            nc.tensor.matmul(S_BANK[c % 2][:, :], ff_w(phase, c * 128, 128), XT[:, par, :],
                                             start=True, stop=True).then_inc(sem["fc1_psum"], 1)
                        else:
                            wait(pe, *at("hid_done", phase, g, NC * unit + c - NC + 1))
                            nc.tensor.matmul((T_BANK[0], S_BANK[0], T_BANK[1], S_BANK[1])[c][:, :],
                                             ff_w(phase, e * 2 * F + c * 128, 128), XT[:, par, :],
                                             start=True, stop=True).then_inc(sem["fc1_psum"], 1)

                def fc2(g, e, par):
                    unit = e if kind == "moe" else 0
                    up = e % 2 if kind == "moe" else par
                    first_col = (2 * F if kind == "geglu" else e * 2 * F + F)
                    wait(pe, *at("hid_done", phase, g, NC * (unit + 1)))
                    if kind == "moe":
                        wait(pe, *at("y_read", phase, g, GB * (unit - 1)))
                    elif kind == "ffn":
                        wait(pe, *at("y_read", phase, g - 1))
                    for b in range(GB):
                        for c in range(NC):
                            last = nc.tensor.matmul((O_BANK, M_BANK)[up][:, b * D:(b + 1) * D],
                                                    PT[:, up, 4 * c + b, :],
                                                    ff_w(phase, first_col + c * D, D), start=c == 0, stop=c == NC - 1,
                                                    skip_group_check=True)
                    last.then_inc(sem["y_psum"], 1)

                if layer < 3:
                    pe.wait_ge(sem[f"w_loaded{layer + 1}"], 16)
                wait(pe, *at("exp_done", phase))
                wait(pe, *at("max_read", phase))

                def emit(g, par, first, last):
                    for e in range(E if kind == "moe" else 1):
                        fc1(g, e, par)
                        if not last and (kind != "moe" or e == 2):
                            wait(pe, *at("xT_ready", phase, g + 1))
                            turn(phase, g + 1)
                        if not last and kind == "moe":
                            if e == 4:
                                route(phase, g + 1, 1 - par)
                            if e == 5:
                                route_turn(phase, g + 1, 1 - par)
                            if e == 6:
                                route_bias(phase, g + 1)
                        if first and not e:
                            wait(pe, *x_done(phase - 1, NG))
                        if last and kind == "moe" and 1 <= e <= len(LEAD_IN):
                            lead_in(attention, phase, e - 1)
                        if last and kind != "moe":
                            lead_in(attention, phase, 0, 1, 2)
                        if e:
                            fc2(g, e - 1, par)
                        elif not first:
                            fc2(g - 1, E - 1 if kind == "moe" else 0, 1 - par)
                    if last:
                        if kind != "moe":
                            lead_in(attention, phase, 3)
                        fc2(g, E - 1 if kind == "moe" else 0, par)
                        if kind != "moe":
                            lead_in(attention, phase, 4)

                feed_steps(pe, emit)

            for phase, (kind, layer) in enumerate(PHASES):
                if kind in ATT:
                    attention_steps(pe, attention, phase)
                else:
                    feed(phase)


def kernel(**inputs):
    import numpy as np
    import concourse.bacc as bacc
    from concourse.bass_utils import run_bass_kernel_spmd

    a = {k: np.asarray(v) for k, v in inputs.items()}
    L = [lambda name, l=l: a[f"L{l}_xattn_{name}"] for l in range(4)]
    order = np.array([(hh * HH + h) * DH + d for hh in range(2) for d in range(DH) for h in range(HH)])

    def att(wq, wk, wv, wo):
        return [wq[:, order], wk[:, order], wv, wo]

    def chunks(w):
        return w.reshape(NC, 128, D).transpose(1, 0, 2).reshape(128, NC * D)

    def in_proj(w):
        return [w[i * D:(i + 1) * D].T for i in range(3)]

    w = []
    w += att(L[0]("Wq1"), L[0]("Wkv1")[:, :D], L[0]("Wkv1")[:, D:], L[0]("Wo1"))
    w += att(L[0]("Wq2"), L[0]("Wkv2")[:, :D], L[0]("Wkv2")[:, D:], L[0]("Wo2"))
    w += [L[0]("Wff1"), chunks(L[0]("Wff2"))]
    w += att(*in_proj(L[1]("sa_in_w")), L[1]("sa_out_w").T)
    w += att(*in_proj(L[1]("ca_in_w")), L[1]("ca_out_w").T)
    for e in range(E):
        w += [L[1]("e_fc1_w")[e].T, chunks(L[1]("e_fc2_w")[e].T)]
    w += att(*in_proj(L[2]("qkv_w")), L[2]("sa_out_w").T)
    w += att(*in_proj(L[2]("ca_in_w")), L[2]("ca_out_w").T)
    w += [L[2]("ff_w1").T, chunks(L[2]("ff_w2").T)]
    w += att(L[3]("Wq_s"), L[3]("Wk_s"), L[3]("Wv_s"), L[3]("proj_s_w"))
    w += att(L[3]("Wq_c"), L[3]("Wk_c"), L[3]("Wv_c"), L[3]("proj_c_w"))
    w += [L[3]("w1"), chunks(L[3]("w2"))]

    cols = np.zeros((128, N_COLS), np.float32)

    def put(name, v):
        c, n = COLS[name]
        cols[:, c:c + n] = v.reshape(n, 128).T

    for l, (g, b) in enumerate((("ln1_s ln2_s ln3_s", "ln1_b ln2_b ln3_b"), ("sa_ln_g ca_q_ln_g moe_ln_g", "sa_ln_b ca_q_ln_b moe_ln_b"),
                                ("n1_g n2_g n3_g", "n1_b n2_b n3_b"), ("ln1_g ln2_g ln3_g", "ln1_b ln2_b ln3_b"))):
        for k, gn, bn in zip("sqf", g.split(), b.split()):
            put(f"g{l}{k}", L[l](gn))
            put(f"b{l}{k}", L[l](bn))
    put("g1c", L[1]("ca_kv_ln_g"))
    put("b1c", L[1]("ca_kv_ln_b"))
    for tag, bias in (("1s", L[1]("sa_in_b")), ("1q", L[1]("ca_in_b")), ("2q", L[2]("ca_in_b"))):
        put("bq" + tag, bias[:D][order])
        put("bk" + tag, bias[D:2 * D][order])
    put("h0", L[0]("bff1"))
    put("h1", L[1]("e_fc1_b"))
    put("h2", L[2]("ff_b1"))
    put("h3", L[3]("b1"))
    put("r1", L[2]("r_b1"))
    put("r2", np.broadcast_to(L[2]("r_b2"), (128,)))
    put("router", np.repeat(L[1]("router_b"), 128))
    put("iota", np.repeat(np.arange(E, dtype=np.float32), 128))
    put("router_w", L[1]("router_w"))

    bias_rows = {"bv1s": L[1]("sa_in_b")[2 * D:], "bv1q": L[1]("ca_in_b")[2 * D:], "bv2q": L[2]("ca_in_b")[2 * D:],
                 "bo0s": L[0]("bo1"), "bo0q": L[0]("bo2"), "bo1s": L[1]("sa_out_b"), "bo1q": L[1]("ca_out_b"),
                 "bo2s": L[2]("sa_out_b"), "bo2q": L[2]("ca_out_b"), "bo3s": L[3]("proj_s_b"), "bo3q": L[3]("proj_c_b"),
                 "f0": L[0]("bff2"), "f2": L[2]("ff_b2"), "f3": L[3]("b2")}
    rows = np.ascontiguousarray(np.broadcast_to(np.stack([bias_rows[n] for n in ROWS_BC]), (128, len(ROWS_BC), D)))
    at = np.arange(128)
    tiles = np.zeros((128, len(TILES), D), np.float32)
    tiles[:, 0] = np.eye(128)
    tiles[:, 1] = np.where(at[None, :] > at[:, None], NEVER, 0.0)
    tiles[:, 2] = tiles[:, 1].T
    tiles[:, 3] = L[2]("r_w1").T[order]
    tiles[:, 4] = np.broadcast_to(L[2]("r_w2").reshape(128, 1), (128, 128))
    tiles[:E, 5] = L[1]("e_fc2_b")

    arrays = {"x": a["x"], "ctx": a["ctx_1024"], "weights": np.concatenate(w, axis=1), "cols": cols, "rows": rows, "tiles": tiles}
    nc = bacc.Bacc("TRN2", target_bir_lowering=False, num_devices=1)
    args = []
    for name in arrays:
        arrays[name] = np.ascontiguousarray(arrays[name])
        args.append(nc.dram_tensor(name, arrays[name].shape, mybir.dt.from_np(arrays[name].dtype), kind="ExternalInput").ap())
    out = nc.dram_tensor("out", (B, S, D), F32, kind="ExternalOutput").ap()
    xattn_kernel(nc, *args, out)
    r = run_bass_kernel_spmd(nc, [arrays], core_ids=[0])
    return r.results[0]["out"]
```
